# Optimizing a Trainium2 kernel written in Bass

```python
import numpy as np
import jax
import jax.numpy as jnp

def _softmax(x, axis=-1):
    return jax.nn.softmax(x, axis=axis)

def _gelu(x):
    return jax.nn.gelu(x, approximate=True)

def _silu(x):
    return jax.nn.silu(x)

def _sigmoid(x):
    return jax.nn.sigmoid(x)

def _layernorm(x, axis=-1, eps=1e-05):
    m = jnp.mean(x, axis=axis, keepdims=True)
    v = jnp.var(x, axis=axis, keepdims=True)
    return (x - m) / jnp.sqrt(v + eps)

def _scatter_add(tgt, idx, src, axis=0):
    return tgt.at[idx].add(src)

def _segment_sum(src, seg, n):
    return jax.ops.segment_sum(src, seg, n)
kernel_name = 'mk_seq_postln_d1_jaxref_r8_549e9b'

def setup_inputs(seed: int=0):
    np.random.seed(seed)
    _w = jnp.asarray

    def _L0_attn_setup():
        import jax, jax.numpy as jnp
        import numpy as np
        HEAD_NUM = 16
        NEG_BIG = 1000000.0
        key = jax.random.key(seed)
        ks = jax.random.split(key, 5)
        E = 128
        B, S = (1, 512)
        x = jax.random.normal(ks[0], (B, S, E), dtype=jnp.float32)
        W1 = jax.random.normal(ks[1], (E, 3 * E), dtype=jnp.float32) * (1.0 / np.sqrt(E))
        b1 = jax.random.normal(ks[2], (3 * E,), dtype=jnp.float32) * 0.02
        Wp = jax.random.normal(ks[3], (E, E), dtype=jnp.float32) * (1.0 / np.sqrt(E))
        bp = jax.random.normal(ks[4], (E,), dtype=jnp.float32) * 0.02
        return {'x': x, 'W1': W1, 'b1': b1, 'Wp': Wp, 'bp': bp}
    _L0_attn_in = _L0_attn_setup()

    def _L0_ffn_setup():
        import jax, jax.numpy as jnp
        import numpy as np
        DIM = 128

        def _reference_tuple_inner(x, W_r, W_k, W_v, mu_r, mu_k):
            B, T, C = x.shape
            x_prev = jnp.concatenate([jnp.zeros((B, 1, C), x.dtype), x[:, :-1, :]], axis=1)
            xr = mu_r * x + (1.0 - mu_r) * x_prev
            xk = mu_k * x + (1.0 - mu_k) * x_prev
            r = jax.nn.sigmoid(jnp.einsum('btc,dc->btd', xr, W_r))
            k = jnp.einsum('btc,dc->btd', xk, W_k)
            k_act = jnp.square(jax.nn.relu(k))
            out = r * jnp.einsum('btc,dc->btd', k_act, W_v)
            new_state = x[:, -1, :]
            return (out, new_state)
        key = jax.random.key(seed)
        ks = jax.random.split(key, 6)
        B, T, C = (8, 256, DIM)
        x = jax.random.normal(ks[0], (B, T, C), dtype=jnp.float32)
        s = 1.0 / np.sqrt(C)
        W_r = jax.random.uniform(ks[1], (C, C), jnp.float32, -s, s)
        W_k = jax.random.uniform(ks[2], (C, C), jnp.float32, -s, s)
        W_v = jax.random.uniform(ks[3], (C, C), jnp.float32, -s, s)
        mu_r = jax.random.uniform(ks[4], (C,), jnp.float32)
        mu_k = jax.random.uniform(ks[5], (C,), jnp.float32)
        return {'x': x, 'W_r': W_r, 'W_k': W_k, 'W_v': W_v, 'mu_r': mu_r, 'mu_k': mu_k}
    _L0_ffn_in = _L0_ffn_setup()
    _d = {'L0_attn_x': _L0_attn_in['x'], 'L0_attn_W1': _L0_attn_in['W1'], 'L0_attn_b1': _L0_attn_in['b1'], 'L0_attn_Wp': _L0_attn_in['Wp'], 'L0_attn_bp': _L0_attn_in['bp'], 'L0_ffn_W_r': _L0_ffn_in['W_r'], 'L0_ffn_W_k': _L0_ffn_in['W_k'], 'L0_ffn_W_v': _L0_ffn_in['W_v'], 'L0_ffn_mu_r': _L0_ffn_in['mu_r'], 'L0_ffn_mu_k': _L0_ffn_in['mu_k']}
    _x0 = _d['L0_attn_x']
    _d['L0_attn_x'] = jax.random.normal(jax.random.fold_in(jax.random.key(seed), 1), (16, 512, 128), dtype=_x0.dtype)
    del _x0
    return _d

def reference(L0_attn_x, L0_attn_W1, L0_attn_b1, L0_attn_Wp, L0_attn_bp, L0_ffn_W_r, L0_ffn_W_k, L0_ffn_W_v, L0_ffn_mu_r, L0_ffn_mu_k):

    def _L0_attn_ref(x, W1, b1, Wp, bp):
        import jax, jax.numpy as jnp
        import numpy as np
        HEAD_NUM = 16
        NEG_BIG = 1000000.0
        B, S, E = x.shape
        H = HEAD_NUM
        d = E // H
        dk = jnp.asarray(d, x.dtype) ** 0.5
        h = x @ W1 + b1
        h = jnp.swapaxes(h.reshape(B, S, H, 3 * d), 1, 2)
        q, k, v = (h[..., :d], h[..., d:2 * d], h[..., 2 * d:])
        w = jnp.einsum('bhqd,bhkd->bhqk', q, k) / dk
        mask = jnp.tril(jnp.ones((S, S), dtype=x.dtype))
        w = jax.nn.softmax(w * mask - (1.0 - mask) * NEG_BIG, axis=-1)
        a = jnp.einsum('bhqk,bhkd->bhqd', w, v)
        a = jnp.swapaxes(a, 1, 2).reshape(B, S, E)
        return a @ Wp + bp

    def _L0_ffn_ref(x, W_r, W_k, W_v, mu_r, mu_k):
        import jax, jax.numpy as jnp
        import numpy as np
        DIM = 128

        def _reference_tuple_inner(x, W_r, W_k, W_v, mu_r, mu_k):
            B, T, C = x.shape
            x_prev = jnp.concatenate([jnp.zeros((B, 1, C), x.dtype), x[:, :-1, :]], axis=1)
            xr = mu_r * x + (1.0 - mu_r) * x_prev
            xk = mu_k * x + (1.0 - mu_k) * x_prev
            r = jax.nn.sigmoid(jnp.einsum('btc,dc->btd', xr, W_r))
            k = jnp.einsum('btc,dc->btd', xk, W_k)
            k_act = jnp.square(jax.nn.relu(k))
            out = r * jnp.einsum('btc,dc->btd', k_act, W_v)
            new_state = x[:, -1, :]
            return (out, new_state)
        return _reference_tuple_inner(x, W_r, W_k, W_v, mu_r, mu_k)[0]
    x = L0_attn_x
    x = _layernorm(x + _L0_attn_ref(x, L0_attn_W1, L0_attn_b1, L0_attn_Wp, L0_attn_bp), axis=-1)
    x = _layernorm(x + _L0_ffn_ref(x, L0_ffn_W_r, L0_ffn_W_k, L0_ffn_W_v, L0_ffn_mu_r, L0_ffn_mu_k), axis=-1)
    return x

_drawn_inputs = setup_inputs


def setup_inputs(seed=0):
    import zlib

    import numpy as np

    out = dict(_drawn_inputs(seed))
    spreads = {}
    factors = {'L0_attn_b1': 3.065, 'L0_attn_bp': 2.784, 'L0_ffn_W_r': 3.182, 'L0_ffn_mu_r': 6.298}
    for name, (base, spread) in spreads.items():
        noise = np.random.default_rng([zlib.crc32(name.encode()), seed]).standard_normal(out[name].shape)
        drawn = base * np.exp(spread * noise) if base else spread * noise
        out[name] = jnp.asarray(drawn.astype(out[name].dtype))
    for name, factor in factors.items():
        out[name] = (out[name] * factor).astype(out[name].dtype)
    return out
```

```python
from contextlib import ExitStack

import concourse.bass as bass
from concourse import mybir

F32 = mybir.dt.float32
BF16 = mybir.dt.bfloat16
ACT = mybir.ActivationFunctionType
ALU = mybir.AluOpType
AX_X = mybir.AxisListType.X

P = 128
BATCH, SEQ, E = 16, 512, 128
HEADS, DH = 16, 8
PAIRS = HEADS // 2
BLK = 64
NBLK = SEQ // BLK
TT = SEQ // P
CHUNKS = NBLK // 2 + 1
GROUPS = 2 * CHUNKS
QUARTET = 4
TERMS = 6 * DH
MROWS = 2
LEADING = 3 * DH
PARTS = 3
EPS = 1e-5
MASKED = -1e30
SCALE = DH ** -0.5

C_IDENT, C_SUMS, C_DUP, C_MASK, C_END = 0, 128, 256, 384, 448

OFFSET = {"X": 3, "A": 2, "S": 1, "T": 0, "D": -1, "E": -2}
FIRST_STEP, LOOP_FROM, LOOP_TO, LAST_STEP = -3, 2, 12, 17

SPARE_USES = {
    (0, 0): ("T", "max1"), (0, 1): ("A", "xT"),
    (1, 0): ("A", "q"), (1, 1): ("A", "k"),
    (2, 0): ("E", "key"), (2, 1): ("D", "sums0"),
    (3, 0): ("E", "gate"), (3, 1): ("D", "sums1"),
    (4, 0): ("E", "value"), (4, 1): ("A", "v"),
    (5, 0): ("S", "max0"),
    (6, 0): ("D", "project"),
    (8, 0): ("D", "hT"),
}


def is_static(b):
    return isinstance(b, int)


def active(stage, b):
    return not is_static(b) or 0 <= b + OFFSET[stage] < BATCH


def before(stage, b):
    n = b + OFFSET[stage]
    return min(max(n, 0), BATCH) if is_static(b) else n


def spare_before(b, name=None):
    n = 0
    for stage in ("A", "S", "T", "D", "E"):
        uses = sum(s == stage for s, _ in SPARE_USES.values())
        n = n + uses * before(stage, b)
    for _, (stage, use) in sorted(SPARE_USES.items()):
        if use == name:
            break
        if name is not None and active(stage, b):
            n = n + 1
    return n


def max_chunk(c):
    if c == 0 or c == CHUNKS - 1:
        return [(NBLK - 1 - c, 0, BLK * (NBLK - c))]
    return [(NBLK - 1 - c, 0, BLK * (NBLK - c)), (c - 1, BLK * (NBLK - c), BLK * c)]


def exp_chunk(c):
    if c == 0 or c == CHUNKS - 1:
        return [(c, 0, SEQ - BLK * c)]
    return [(c, 0, SEQ - BLK * c), (NBLK - c, SEQ - BLK * c, BLK * c)]


def block_program(nc, x, W1, b1, Wp, bp, Wr, Wk, Wv, mu_r, mu_k, consts, out):
    with ExitStack() as ctx:
        def sb(name, shape, dt=F32):
            return ctx.enter_context(nc.sbuf_tensor(name, shape, dt))

        def ps(name, shape):
            return ctx.enter_context(nc.psum_tensor(name, shape, F32))

        def sem(name):
            return ctx.enter_context(nc.semaphore(name))

        cst = sb("cst", [P, C_END])
        ident = cst[:, C_IDENT:C_IDENT + P]
        sums_sel = cst[:, C_SUMS:C_SUMS + P]
        dup = sb("dup", [BLK, P], BF16)
        qmask = sb("qmask", [BLK, BLK], BF16)
        w1 = sb("w1", [E, 3 * E])
        w1p = sb("w1p", [E, 3, E])
        wff = sb("wff", [E, 3, E])
        wffT = sb("wffT", [E, 3, E])
        wpp = sb("wpp", [P, 2, E])
        rows = sb("rows", [1, 4 * E])
        rowsp = sb("rowsp", [1, 3, E])
        ones = sb("ones", [1, P])
        bias = sb("bias", [P, 3 * E])
        mus = sb("mus", [P, 2])
        half_power = sb("half_power", [P, TT])
        xa = sb("xa", [P, 2, TT, E])
        xT = sb("xT", [P, SEQ])
        qk = sb("qk", [P, 2, SEQ])
        qk_rest = sb("qk_rest", [P, 2, SEQ])
        qk_parts = sb("qk_parts", [P, 2 * PARTS, SEQ], BF16)
        vnat = sb("vnat", [P, TT, 2, DH * PAIRS])
        qop = sb("qop", [P, 2, PAIRS, SEQ], BF16)
        kop = sb("kop", [P, 2, PAIRS, SEQ], BF16)
        vop = sb("vop", [P, 2, NBLK, 4, DH, PAIRS])
        rowmax = sb("rowmax", [P, 2, PAIRS, NBLK])
        negmax = sb("negmax", [QUARTET * NBLK, P])
        negmax_parts = sb("negmax_parts", [QUARTET * NBLK, MROWS, P], BF16)
        probs = sb("probs", [P, 2, QUARTET, SEQ])
        osum = sb("osum", [P, 2, SEQ])
        inv = sb("inv", [P, 2, SEQ])
        attn = sb("attn", [P, 2, SEQ])
        xres = sb("xres", [P, TT, E])
        xbias = sb("xbias", [P, TT, E])
        y = sb("y", [P, TT, E])
        stats = sb("stats", [P, 2, TT, 6])
        moments = sb("moments", [P, 2, TT, 2])
        vareps = sb("vareps", [P, 2, TT])
        rstd = sb("rstd", [P, 2, TT])
        h = sb("h", [P, 2, TT, E])
        hT = sb("hT", [P, SEQ + 1])
        step_d = sb("step_d", [P, SEQ])
        scaled = sb("scaled", [P, 2, SEQ])
        mixed = sb("mixed", [P, 2, SEQ])
        krelu = sb("krelu", [P, SEQ])
        ksq = sb("ksq", [P, SEQ])
        egate = sb("egate", [P, SEQ])
        egate1 = sb("egate1", [P, SEQ])
        gate = sb("gate", [P, SEQ])
        gated = sb("gated", [P, SEQ])
        z = sb("z", [P, TT, E])
        result = sb("result", [P, TT, E])

        tps = ps("tps", [P, 2, SEQ])
        sps = ps("sps", [P, 2, 2, SEQ])
        ops = ps("ops", [P, SEQ])
        spare = ps("spare", [P, SEQ])

        d_parts = nc.dram_tensor("d_parts", (2, 2, 2, PAIRS, DH, PARTS, SEQ), BF16, kind="Internal").ap()
        d_max = nc.dram_tensor("d_max", (2, MROWS, 2, QUARTET * NBLK, BLK), BF16, kind="Internal").ap()

        weights_in = sem("weights_in")
        wpp_cleared = sem("wpp_cleared")
        kop_cleared = sem("kop_cleared")
        vop_cleared = sem("vop_cleared")
        setup_pe = sem("setup_pe")
        setup_act = sem("setup_act")
        setup_dve = sem("setup_dve")
        armed = sem("armed")
        xa_in = sem("xa_in")
        xres_in = sem("xres_in")
        spare_written = sem("spare_written")
        spare_read = sem("spare_read")
        qk_split = sem("qk_split")
        split_step = sem("split_step")
        qk_copied = sem("qk_copied")
        parts_out = sem("parts_out")
        ops_in = [sem("ops_in0"), sem("ops_in1")]
        vop_in = sem("vop_in")
        s_done = sem("s_done")
        s_reduced = sem("s_reduced")
        max_copied = sem("max_copied")
        max_high = sem("max_high")
        max_split = sem("max_split")
        max_out = sem("max_out")
        max_in = [sem("max_in0"), sem("max_in1")]
        t_done = sem("t_done")
        exp_done = sem("exp_done")
        masked_first = sem("masked_first")
        masked = sem("masked")
        pv_done = sem("pv_done")
        o_copied = sem("o_copied")
        inv_done = sem("inv_done")
        attn_done = sem("attn_done")
        xbias_done = sem("xbias_done")
        stats_done = sem("stats_done")
        moments_done = sem("moments_done")
        vareps_done = sem("vareps_done")
        rstd_done = sem("rstd_done")
        h_done = sem("h_done")
        hT_copied = sem("hT_copied")
        step_done = sem("step_done")
        scaled_done = sem("scaled_done")
        mixed_done = sem("mixed_done")
        krelu_done = sem("krelu_done")
        ksq_done = sem("ksq_done")
        egate_done = sem("egate_done")
        egate1_done = sem("egate1_done")
        gate_done = sem("gate_done")
        z_done = sem("z_done")
        stats2_done = sem("stats2_done")
        moments2_done = sem("moments2_done")
        vareps2_done = sem("vareps2_done")
        rstd2_done = sem("rstd2_done")
        result_done = sem("result_done")
        stored = sem("stored")

        def wait(eng, semaphore, value, alone=True):
            if is_static(value):
                if value > 0:
                    eng.wait_ge(semaphore, value)
            else:
                value = eng.to_reg(value)
                if alone:
                    eng.wait_ge(armed, 1)
                eng.wait_ge(semaphore, value)

        def run_steps(eng, step):
            for b in range(FIRST_STEP, LOOP_FROM):
                step(b, b % 2)
            with eng.Fori(LOOP_FROM, LOOP_TO, 2) as b:
                step(b, LOOP_FROM % 2)
                step(b + 1, (LOOP_FROM + 1) % 2)
            for b in range(LOOP_TO, LAST_STEP + 1):
                step(b, b % 2)

        block = ctx.enter_context(nc.Block())

        @block.sync
        def _(sp):
            for dst, src in (
                (cst[:], consts),
                (w1[:], W1),
                (wff[:, 0, :], Wr), (wff[:, 1, :], Wk), (wff[:, 2, :], Wv),
                (rows[:, 0:3 * E], b1.rearrange("(o n) -> o n", o=1)),
                (rows[:, 3 * E:], bp.rearrange("(o n) -> o n", o=1)),
                (mus[:, 0:1], mu_r.rearrange("(n o) -> n o", o=1)),
                (mus[:, 1:2], mu_k.rearrange("(n o) -> n o", o=1)),
            ):
                sp.dma_start(dst, src).then_inc(weights_in, 16)
            sp.wait_ge(wpp_cleared, 1)
            for half in range(2):
                for t in range(QUARTET):
                    r = (half * QUARTET + t) * 2 * DH
                    sp.dma_start(wpp[32 * t:32 * t + 2 * DH, half, :], Wp[r:r + 2 * DH, :]).then_inc(weights_in, 16)

            def load_operands(n, batch, par, half):
                prs = slice(QUARTET * half, QUARTET * half + QUARTET)
                for hh in range(2):
                    r = BLK * hh
                    for qk_i, operand, order in ((0, qop, (0, 0, 1)), (1, kop, (2, 1, 2))):
                        src = d_parts[par, qk_i, hh, prs]
                        for i, part in enumerate(order):
                            sp.dma_start(operand[r + DH * i:r + DH * i + DH, par, prs, :],
                                         src[:, :, part, :].rearrange("p d n -> d p n")).then_inc(ops_in[half], 16)
                        sp.dma_start(operand[r + LEADING:r + TERMS, par, prs, :],
                                     src.rearrange("p d t n -> (d t) p n")).then_inc(ops_in[half], 16)

            def load_max(b, stage, par, half, count):
                wait(sp, max_split, count + 1)
                sp.dma_start(d_max[half].rearrange("i h r q -> r i h q"),
                             negmax_parts[:].rearrange("r i (h q) -> r i h q", h=2)).then_inc(max_out, 16)
                wait(sp, max_out, 16 * (count + 1))
                for hh in range(2):
                    r = BLK * hh + TERMS
                    sp.dma_start(qop[r:r + MROWS, par, QUARTET * half:QUARTET * half + QUARTET, :],
                                 d_max[half, :, hh].rearrange("i r q -> i (r q)")).then_inc(max_in[half], 16)

            def step(b, par):
                other = 1 - par
                if active("S", b):
                    wait(sp, parts_out, 16 * before("A", b))
                    wait(sp, t_done, 4 * GROUPS * before("T", b))
                    wait(sp, s_done, 2 * GROUPS * before("S", b))
                    load_operands(b, None, other, 1)
                if active("T", b):
                    load_max(b, "T", par, 1, 2 * before("T", b) + 1)
                if active("S", b):
                    wait(sp, pv_done, GROUPS * before("T", b) + (1 if active("T", b) else 0))
                    wait(sp, spare_read, spare_before(b))
                    wait(sp, vop_in, 64 * before("S", b))
                    for half in range(2):
                        for hh in range(2):
                            sp.dma_start(
                                vop[BLK * hh:BLK * hh + BLK, other, :, hh].rearrange(
                                    "k (t two) d p -> k two t (d p)", two=2)[:, half],
                                vnat[BLK * half:BLK * half + BLK, :, hh, :]).then_inc(vop_in, 16)
                if active("X", b):
                    wait(sp, spare_written, spare_before(b, "xT") + 1 if active("A", b) else spare_before(b))
                    wait(sp, xa_in, 16 * before("X", b))
                    sp.dma_start(xa[:, other], x[b + OFFSET["X"]].rearrange("(t p) e -> p t e", p=P)).then_inc(xa_in, 16)
                if active("D", b):
                    wait(sp, xbias_done, before("D", b))
                    sp.dma_start(xres[:], x[b + OFFSET["D"]].rearrange("(t p) e -> p t e", p=P)).then_inc(xres_in, 16)
                if active("A", b):
                    wait(sp, qk_split, before("A", b) + 1)
                    wait(sp, ops_in[0], 256 * before("A", b))
                    wait(sp, ops_in[1], 256 * before("S", b))
                    sp.dma_start(d_parts[par].rearrange("k h p d t n -> (h p d) k t n"),
                                 qk_parts[:].rearrange("r (k t) n -> r k t n", k=2)).then_inc(parts_out, 16)
                if active("S", b):
                    load_max(b, "S", other, 0, 2 * before("S", b))
                if active("A", b):
                    wait(sp, parts_out, 16 * (before("A", b) + 1))
                    if active("T", b):
                        wait(sp, t_done, 4 * GROUPS * before("T", b) + 4 * CHUNKS)
                    if active("S", b):
                        wait(sp, s_done, 2 * GROUPS * before("S", b) + GROUPS)
                    load_operands(b, None, par, 0)
                if active("E", b):
                    wait(sp, result_done, before("E", b) + 1)
                    sp.dma_start(out[b + OFFSET["E"]].rearrange("(t p) e -> p t e", p=P), result[:]).then_inc(stored, 16)

            sp.wait_ge(kop_cleared, 1)
            sp.wait_ge(vop_cleared, 2)
            run_steps(sp, step)
            sp.wait_ge(stored, 16 * BATCH)

        @block.tensor
        def _(pe):
            pe.wait_ge(weights_in, 16 * 17)
            for i in range(3):
                last = nc.tensor.transpose(spare[:, E * i:E * i + E], wff[:, i, :], ident)
            last.then_inc(setup_pe, 1)
            pe.wait_ge(setup_act, 1)
            pe.wait_ge(setup_dve, 1)
            for i in range(2):
                nc.tensor.matmul(spare[:, i:i + 1], rowsp[:, i, :], ones[:, 0:1], start=True, stop=True)
            nc.tensor.matmul(spare[:, E:2 * E], ones[:], rowsp[:, 2, :], start=True, stop=True)
            nc.tensor.matmul(spare[:, 2 * E:3 * E], ones[:], rows[:, 3 * E:], start=True, stop=True).then_inc(setup_pe, 1)
            pe.wait_ge(setup_act, 2)
            pe.wait_ge(armed, 1)

            def rowmax_transpose(par, half):
                src = rowmax[:, par, QUARTET * half:QUARTET * half + QUARTET, :].rearrange("p a b -> p (a b)")
                return nc.tensor.transpose(spare[0:QUARTET * NBLK, 0:P], src, ident)

            def tokens_by_weights(tokensT, weights):
                for t in range(TT):
                    last = nc.tensor.matmul(spare[:, P * t:P * t + P], tokensT[:, P * t:P * t + P], weights,
                                            start=True, stop=True)
                return last

            def spare_use(b, par, g, place):
                stage, use = SPARE_USES.get((g, place), (None, None))
                if stage is None or not active(stage, b):
                    return
                wait(pe, spare_read, spare_before(b, use))
                if use == "xT":
                    wait(pe, xa_in, 16 * (before("A", b) + 1))
                    for t in range(TT):
                        last = nc.tensor.transpose(spare[:, P * t:P * t + P], xa[:, par, t, :], ident)
                elif use in ("q", "k"):
                    last = nc.tensor.matmul(spare[:], w1p[:, "qk".index(use), :], xT[:], start=True, stop=True)
                elif use == "v":
                    last = tokens_by_weights(xT, w1p[:, 2, :])
                elif use == "max0":
                    wait(pe, s_reduced, 2 * GROUPS * before("S", b) + GROUPS)
                    last = rowmax_transpose(1 - par, 0)
                elif use == "max1":
                    wait(pe, s_reduced, 2 * GROUPS * (before("T", b) + 1))
                    last = rowmax_transpose(par, 1)
                elif use in ("sums0", "sums1"):
                    half = int(use[-1])
                    wait(pe, o_copied, 2 * before("D", b) + half + 1)
                    last = nc.tensor.matmul(spare[:], sums_sel, osum[:, half, :], start=True, stop=True)
                elif use == "project":
                    wait(pe, attn_done, 2 * (before("D", b) + 1))
                    for t in range(TT):
                        for half in range(2):
                            last = nc.tensor.matmul(spare[:, P * t:P * t + P], attn[:, half, P * t:P * t + P],
                                                    wpp[:, half, :], start=half == 0, stop=half == 1)
                elif use == "hT":
                    wait(pe, h_done, before("D", b) + 1)
                    for t in range(TT):
                        last = nc.tensor.transpose(spare[:, P * t:P * t + P], h[:, 1 - par, t, :], ident)
                elif use == "key":
                    wait(pe, mixed_done, 2 * (before("E", b) + 1))
                    last = nc.tensor.matmul(spare[:], wffT[:, 1, :], mixed[:, 1, :], start=True, stop=True)
                elif use == "gate":
                    last = tokens_by_weights(mixed[:, 0], wffT[:, 0, :])
                elif use == "value":
                    wait(pe, ksq_done, before("E", b) + 1)
                    last = tokens_by_weights(ksq, wffT[:, 2, :])
                last.then_inc(spare_written, 1)

            def t_chunk(b, par, g, i):
                n = 4 * GROUPS * before("T", b) + 4 * g + i
                half, c = divmod(g, CHUNKS)
                if c == 0 and i == 0:
                    wait(pe, max_in[half], 32 * (before("T", b) + 1))
                wait(pe, exp_done, n - 1)
                pair = QUARTET * half + i
                for a, off, w in exp_chunk(c):
                    for hh in range(2):
                        r = slice(BLK * hh, BLK * hh + TERMS + MROWS)
                        last = nc.tensor.matmul(tps[BLK * hh:BLK * hh + BLK, i % 2, off:off + w],
                                                kop[r, par, pair, BLK * a:BLK * a + BLK],
                                                qop[r, par, pair, BLK * a:SEQ], start=True, stop=True)
                last.then_inc(t_done, 1)

            def s_chunk(b, par, g, i):
                n = 2 * GROUPS * before("S", b) + 2 * g + i
                half, c = divmod(g, CHUNKS)
                if c == 0 and i == 0:
                    wait(pe, ops_in[half], 256 * (before("S", b) + 1))
                wait(pe, s_reduced, n - 1)
                for k in range(2):
                    pair = QUARTET * half + 2 * i + k
                    blocks = max_chunk(c)
                    for j, (a, off, w) in enumerate(blocks):
                        for hh in range(2):
                            r = slice(BLK * hh, BLK * hh + LEADING)
                            nc.tensor.matmul(sps[BLK * hh:BLK * hh + BLK, i, k, off:off + w],
                                             qop[r, par, pair, BLK * a:BLK * a + BLK],
                                             kop[r, par, pair, 0:w], start=j == 0, stop=False,
                                             skip_group_check=True)
                    for j, (a, off, w) in enumerate(blocks):
                        last = nc.tensor.matmul(sps[:, i, k, off + w - BLK:off + w], dup[:], qmask[:],
                                                start=False, stop=j == len(blocks) - 1, skip_group_check=True)
                last.then_inc(s_done, 1)

            def pv(entries, par, g):
                half, c = divmod(g, CHUNKS)
                if c == 0:
                    wait(pe, o_copied, 2 * entries + half)
                    if half == 0:
                        wait(pe, vop_in, 64 * (entries + 1))
                wait(pe, masked, GROUPS * entries + g + 1)
                blocks = exp_chunk(c)
                for a, off, w in blocks:
                    for t in range(QUARTET):
                        last = nc.tensor.matmul(ops[32 * t:32 * t + 32, BLK * a:SEQ],
                                                vop[:, par, a, :, :, QUARTET * half + t].rearrange("k s d -> k (s d)"),
                                                probs[:, g % 2, t, off:off + w],
                                                start=c == 0, stop=c == CHUNKS - 1, skip_group_check=True)
                last.then_inc(pv_done, 1)

            def step(b, par):
                for g in range(GROUPS):
                    if active("T", b):
                        t_chunk(b, par, g, 0)
                        t_chunk(b, par, g, 1)
                    spare_use(b, par, g, 0)
                    if active("S", b):
                        s_chunk(b, 1 - par, g, 0)
                    if active("T", b):
                        t_chunk(b, par, g, 2)
                        t_chunk(b, par, g, 3)
                    if active("S", b):
                        s_chunk(b, 1 - par, g, 1)
                    if g == 0 and active("D", b):
                        pv(before("D", b), 1 - par, GROUPS - 1)
                    elif g > 0 and active("T", b):
                        pv(before("T", b), par, g - 1)
                    spare_use(b, par, g, 1)

            run_steps(pe, step)

        @block.scalar
        def _(act):
            act.wait_ge(setup_pe, 1)
            nc.scalar.copy(wffT[:].rearrange("p a b -> p (a b)"), spare[:, 0:3 * E]).then_inc(setup_act, 1)
            act.wait_ge(setup_pe, 2)
            nc.scalar.copy(bias[:, 0:2], spare[:, 0:2])
            nc.scalar.copy(bias[:, E:3 * E], spare[:, E:3 * E]).then_inc(setup_act, 1)
            act.wait_ge(setup_act, 2)
            act.wait_ge(armed, 1)

            def spare_use(b, par, g, place):
                stage, use = SPARE_USES.get((g, place), (None, None))
                if stage is None or not active(stage, b) or use in ("v", "sums0", "sums1", "project", "value"):
                    return
                n = before(stage, b)
                if use in ("max0", "max1"):
                    m = 2 * n + (0 if use == "max0" else 1)
                    wait(act, max_split, m)
                wait(act, spare_written, spare_before(b, use) + 1)
                if use == "xT":
                    ins = nc.scalar.copy(xT[:], spare[:])
                elif use in ("q", "k"):
                    i = "qk".index(use)
                    wait(act, qk_split, n)
                    ins = nc.scalar.activation(qk[:, i, :], spare[:], ACT.Identity, bias=bias[:, i:i + 1])
                elif use in ("max0", "max1"):
                    ins = nc.scalar.activation(negmax[:], spare[0:QUARTET * NBLK, 0:P], ACT.Copy, scale=-1.0)
                elif use == "hT":
                    wait(act, mixed_done, 2 * n)
                    ins = nc.scalar.copy(hT[:, 1:SEQ + 1], spare[:])
                elif use == "key":
                    wait(act, ksq_done, n)
                    ins = nc.scalar.activation(krelu[:], spare[:], ACT.Relu)
                elif use == "gate":
                    wait(act, egate1_done, n)
                    ins = nc.scalar.activation(egate[:], spare[:], ACT.Exp, scale=-1.0)
                ins.then_inc(spare_read, 1)

            def exp_chunk_of(b, g, i):
                n = before("T", b)
                half, c = divmod(g, CHUNKS)
                if i == 0:
                    wait(act, pv_done, GROUPS * n + g - 1)
                wait(act, t_done, 4 * GROUPS * n + 4 * g + i + 1)
                w = SEQ if c < CHUNKS - 1 else SEQ // 2
                nc.scalar.activation(probs[:, g % 2, i, 0:w], tps[:, i % 2, 0:w], ACT.Exp, scale=SCALE)\
                    .then_inc(exp_done, 1)

            def copy_o(n, half):
                wait(act, attn_done, 2 * n + half - 1)
                wait(act, pv_done, GROUPS * n + CHUNKS * (half + 1))
                nc.scalar.copy(osum[:, half, :], ops[:]).then_inc(o_copied, 1)

            def step(b, par):
                for g in range(GROUPS):
                    if active("T", b):
                        exp_chunk_of(b, g, 0)
                        exp_chunk_of(b, g, 1)
                    spare_use(b, par, g, 0)
                    if active("T", b):
                        exp_chunk_of(b, g, 2)
                        exp_chunk_of(b, g, 3)
                    if g == 0 and active("D", b):
                        copy_o(before("D", b), 1)
                    if g == CHUNKS and active("T", b):
                        copy_o(before("T", b), 0)
                    spare_use(b, par, g, 1)

            run_steps(act, step)

        @block.vector
        def _(dve):
            nc.vector.memset(wpp[:], 0.0).then_inc(wpp_cleared, 1)
            nc.vector.memset(ones[:], 1.0)
            nc.vector.memset(kop[:], 1.0).then_inc(kop_cleared, 1)
            nc.vector.memset(hT[:, 0:1], 0.0)
            dve.wait_ge(vop_cleared, 1)
            for par in range(2):
                for hh in range(2):
                    last = nc.vector.memset(vop[BLK * hh:BLK * hh + BLK, par, :, 2 + hh], 1.0)
            last.then_inc(vop_cleared, 1)
            dve.wait_ge(weights_in, 16 * 17)
            nc.vector.tensor_copy(dup[:], cst[0:BLK, C_DUP:C_DUP + P])
            nc.vector.tensor_copy(qmask[:], cst[0:BLK, C_MASK:C_MASK + BLK])
            for i in range(3):
                order = "c (h p d) -> c h p d" if i < 2 else "c (h d p) -> c h p d"
                nc.vector.tensor_copy(
                    w1p[:, i, :].rearrange(order, h=2, d=DH),
                    w1[:].rearrange("c (p h i d) -> c i h p d", h=2, i=3, d=DH)[:, i])
                last = nc.vector.tensor_copy(
                    rowsp[:, i, :].rearrange(order, h=2, d=DH),
                    rows[:, 0:3 * E].rearrange("c (p h i d) -> c i h p d", h=2, i=3, d=DH)[:, i])
            last.then_inc(setup_dve, 1)
            dve.wait_ge(setup_dve, 1)
            dve.wait_ge(setup_act, 2)
            nc.vector.memset(half_power[:], -0.5).then_inc(armed, 1)

            def reduce_chunk(b, par, g, i):
                n = 2 * GROUPS * before("S", b) + 2 * g + i
                half, c = divmod(g, CHUNKS)
                wait(dve, s_done, n + 1, alone=False)
                pairs = slice(QUARTET * half + 2 * i, QUARTET * half + 2 * i + 2)
                for a, off, w in max_chunk(c):
                    last = nc.vector.reduce_max(rowmax[:, par, pairs, a], sps[:, i, :, off:off + w], axis=AX_X)
                last.then_inc(s_reduced, 1)

            def layer_norm_moments(src, i, n, ready, value, done_stats, done_moments):
                wait(dve, ready, value)
                for t in range(TT):
                    last = nc.vector.bn_stats(out=stats[:, i, t, :], in_=src[:, t, :])
                last.then_inc(done_stats, 1)
                wait(dve, done_stats, n + 1)
                for t in range(TT):
                    last = nc.vector.bn_aggr(out=moments[:, i, t, :], in_=stats[:, i, t, :])
                last.then_inc(done_moments, 1)

            def spare_use(b, par, g, place):
                stage, use = SPARE_USES.get((g, place), (None, None))
                if stage is None or not active(stage, b):
                    return
                n = before(stage, b)
                written = spare_before(b, use) + 1
                if use == "v":
                    wait(dve, vop_in, 64 * before("S", b) + (64 if active("S", b) else 0))
                    wait(dve, spare_written, written)
                    nc.vector.tensor_tensor(
                        vnat[:].rearrange("p t h r -> p t (h r)"), spare[:].rearrange("p (t r) -> p t r", t=TT),
                        bias[:, E:2 * E].unsqueeze(1).to_broadcast([P, TT, E]), ALU.add).then_inc(spare_read, 1)
                elif use in ("sums0", "sums1"):
                    half = int(use[-1])
                    wait(dve, spare_written, written)
                    nc.vector.reciprocal(inv[:, half, :], spare[:]).then_inc(spare_read, 1)
                elif use == "project":
                    wait(dve, xbias_done, n + 1)
                    wait(dve, h_done, n)
                    wait(dve, spare_written, written)
                    nc.vector.tensor_tensor(y[:].rearrange("p t e -> p (t e)"), spare[:],
                                            xbias[:].rearrange("p t e -> p (t e)"), ALU.add).then_inc(spare_read, 1)
                elif use == "value":
                    wait(dve, gate_done, n + 1)
                    wait(dve, z_done, n)
                    wait(dve, spare_written, written)
                    nc.vector.tensor_tensor(gated[:], spare[:], gate[:], ALU.mult).then_inc(spare_read, 1)

            def divide(b, half):
                n = before("D", b)
                wait(dve, spare_read, spare_before(b, f"sums{half}") + 1)
                nc.vector.tensor_tensor(attn[:, half, :], osum[:, half, :], inv[:, half, :], ALU.mult)\
                    .then_inc(attn_done, 1)

            def step(b, par):
                for g in range(GROUPS):
                    if active("S", b):
                        reduce_chunk(b, 1 - par, g, 0)
                    if g in (3, 4) and active("D", b):
                        divide(b, g - 3)
                    if g == 6 and active("E", b):
                        layer_norm_moments(z, 1, before("E", b), z_done, before("E", b) + 1, stats2_done, moments2_done)
                    if g == 7 and active("D", b):
                        layer_norm_moments(y, 0, before("D", b), spare_read, spare_before(b, "project") + 1,
                                           stats_done, moments_done)
                    if g == 4 and active("E", b):
                        n = before("E", b)
                        wait(dve, z_done, n)
                        wait(dve, egate1_done, n + 1)
                        nc.vector.reciprocal(gate[:], egate1[:]).then_inc(gate_done, 1)
                    spare_use(b, par, g, 0)
                    if active("S", b):
                        reduce_chunk(b, 1 - par, g, 1)
                    spare_use(b, par, g, 1)

            run_steps(dve, step)

        @block.gpsimd
        def _(pool):
            nc.gpsimd.memset(vop[:], 0.0).then_inc(vop_cleared, 1)
            pool.wait_ge(armed, 1)

            def mask_group(b, g):
                n = before("T", b)
                wait(pool, exp_done, 4 * GROUPS * n + 4 * g + 4)
                for hh in range(2):
                    if hh == 1:
                        wait(pool, masked_first, GROUPS * n + g + 1)
                    for _, off, _ in exp_chunk(g % CHUNKS):
                        v = probs[0:BLK * (hh + 1), g % 2, :, off:off + BLK]
                        last = nc.gpsimd.affine_select(out=v, in_=v, compare_op=ALU.is_ge, fill=0.0, base=BLK * hh,
                                                       pattern=[[0, QUARTET], [1, BLK]], channel_multiplier=-1)
                    last.then_inc((masked_first, masked)[hh], 1)

            def split_qk(b, i):
                n = before("A", b)
                part = lambda t: qk_parts[:, t:2 * PARTS - t:2 * PARTS - 1 - 2 * t, :]
                if i == 0:
                    wait(pool, spare_read, spare_before(b, "k") + 1)
                    wait(pool, parts_out, 16 * n)
                    nc.gpsimd.tensor_copy(part(0), qk[:]).then_inc(split_step, 1)
                    return
                wait(pool, split_step, 3 * n + i)
                if i == 1:
                    nc.gpsimd.tensor_tensor(qk_rest[:], qk[:], part(0), ALU.subtract).then_inc(split_step, 1)
                elif i == 2:
                    nc.gpsimd.tensor_copy(part(1), qk_rest[:]).then_inc(split_step, 1)
                else:
                    nc.gpsimd.tensor_tensor(part(2), qk_rest[:], part(1), ALU.subtract).then_inc(qk_split, 1)

            def split_max(n, b, use):
                wait(pool, spare_read, spare_before(b, use) + 1)
                wait(pool, max_out, 16 * n)
                nc.gpsimd.tensor_copy(negmax_parts[:, 0, :], negmax[:]).then_inc(max_high, 1)
                wait(pool, max_high, n + 1)
                nc.gpsimd.tensor_tensor(negmax_parts[:, 1, :], negmax[:], negmax_parts[:, 0, :], ALU.subtract)\
                    .then_inc(max_split, 1)

            def normalise(i, n, src, dst, done_moments, done_eps, done_rstd, done):
                wait(pool, done_moments, n + 1)
                nc.gpsimd.tensor_scalar(vareps[:, i, :], moments[:, i, :, 1], EPS, None, ALU.add).then_inc(done_eps, 1)
                wait(pool, done_eps, n + 1)
                nc.gpsimd.tensor_tensor(rstd[:, i, :], vareps[:, i, :], half_power[:], ALU.pow).then_inc(done_rstd, 1)
                wait(pool, done_rstd, n + 1)
                for t in range(TT):
                    last = nc.gpsimd.tensor_scalar(dst[:, t, :], src[:, t, :], moments[:, i, t, 0:1],
                                                   rstd[:, i, t:t + 1], ALU.subtract, ALU.mult)
                last.then_inc(done, 1)

            def mix(b):
                n = before("D", b)
                wait(pool, spare_read, spare_before(b, "hT") + 1)
                nc.gpsimd.tensor_tensor(step_d[:], hT[:, 1:SEQ + 1], hT[:, 0:SEQ], ALU.subtract).then_inc(step_done, 1)
                wait(pool, step_done, n + 1)
                for i in range(2):
                    nc.gpsimd.tensor_scalar(scaled[:, i, :], step_d[:], mus[:, i:i + 1], None, ALU.mult)\
                        .then_inc(scaled_done, 1)
                for i in range(2):
                    wait(pool, scaled_done, 2 * n + i + 1)
                    nc.gpsimd.tensor_tensor(mixed[:, i, :], scaled[:, i, :], hT[:, 0:SEQ], ALU.add)\
                        .then_inc(mixed_done, 1)

            def step(b, par):
                for g in range(GROUPS):
                    if active("T", b):
                        mask_group(b, g)
                    if g == 0 and active("T", b):
                        split_max(2 * before("T", b) + 1, b, "max1")
                    if g == 2 and active("E", b):
                        n = before("E", b)
                        wait(pool, spare_read, spare_before(b, "key") + 1)
                        nc.gpsimd.tensor_tensor(ksq[:], krelu[:], krelu[:], ALU.mult).then_inc(ksq_done, 1)
                    if g == 3 and active("E", b):
                        n = before("E", b)
                        wait(pool, spare_read, spare_before(b, "gate") + 1)
                        nc.gpsimd.tensor_scalar(egate1[:], egate[:], 1.0, None, ALU.add).then_inc(egate1_done, 1)
                    if g in (2, 3, 4, 5) and active("A", b):
                        split_qk(b, g - 2)
                    if g == 4 and active("E", b):
                        n = before("E", b)
                        wait(pool, spare_read, spare_before(b, "value") + 1)
                        nc.gpsimd.tensor_tensor(z[:].rearrange("p t e -> p (t e)"), gated[:],
                                                h[:, par].rearrange("p t e -> p (t e)"), ALU.add).then_inc(z_done, 1)
                    if g == 5 and active("S", b):
                        split_max(2 * before("S", b), b, "max0")
                    if g == 5 and active("D", b):
                        n = before("D", b)
                        wait(pool, xres_in, 16 * (n + 1))
                        wait(pool, h_done, n)
                        nc.gpsimd.tensor_tensor(xbias[:], xres[:],
                                                bias[:, 2 * E:3 * E].unsqueeze(1).to_broadcast([P, TT, E]),
                                                ALU.add).then_inc(xbias_done, 1)
                    if g == 6 and active("E", b):
                        n = before("E", b)
                        wait(pool, stored, 16 * n)
                        normalise(1, n, z, result, moments2_done, vareps2_done, rstd2_done, result_done)
                    if g == 7 and active("D", b):
                        normalise(0, before("D", b), y, h[:, 1 - par], moments_done, vareps_done, rstd_done, h_done)
                    if g == 8 and active("D", b):
                        mix(b)

            run_steps(pool, step)


def shape_constants(np):
    c = np.zeros((P, C_END), np.float32)
    c[:, C_IDENT:C_IDENT + P] = np.eye(P)
    for r in range(P):
        c[r + 2 * DH if r % 32 < 2 * DH else r, C_SUMS + r] = 1.0
    c[0:BLK, C_DUP:C_DUP + P] = np.tile(np.eye(BLK), (1, 2))
    c[0:BLK, C_MASK:C_MASK + BLK] = np.triu(np.full((BLK, BLK), MASKED), 1)
    return c


INPUTS = ["L0_attn_x", "L0_attn_W1", "L0_attn_b1", "L0_attn_Wp", "L0_attn_bp",
          "L0_ffn_W_r", "L0_ffn_W_k", "L0_ffn_W_v", "L0_ffn_mu_r", "L0_ffn_mu_k"]


def kernel(**inputs):
    import numpy as np
    import concourse.bacc as bacc
    from concourse.bass_utils import run_bass_kernel_spmd

    nc = bacc.Bacc("TRN2", target_bir_lowering=False, num_devices=1)
    arrays = {name: np.ascontiguousarray(inputs[name]) for name in INPUTS}
    arrays["shape_constants"] = shape_constants(np)
    args = [nc.dram_tensor(name, a.shape, mybir.dt.from_np(a.dtype), kind="ExternalInput").ap()
            for name, a in arrays.items()]
    args.append(nc.dram_tensor("out", (BATCH, SEQ, E), F32, kind="ExternalOutput").ap())
    block_program(nc, *args)
    return run_bass_kernel_spmd(nc, [arrays], core_ids=[0]).results[0]["out"]
```

```python
from contextlib import ExitStack

import concourse.bass as bass
from concourse import mybir

F32 = mybir.dt.float32
BF16 = mybir.dt.bfloat16
ACT = mybir.ActivationFunctionType
ALU = mybir.AluOpType
AX_X = mybir.AxisListType.X

P = 128
BATCH, SEQ, E = 16, 512, 128
HEADS, DH = 16, 8
PAIRS = HEADS // 2
BLK = 128
HROWS = 64
NBLK = SEQ // BLK
TT = SEQ // P
CHUNKS = 5
GROUPS = 2 * CHUNKS
QUARTET = 4
TERMS = 6 * DH
MROWS = 2
LEADING = 3 * DH
MAXIMA = QUARTET * 2 * NBLK
PARTS = 3
EPS = 1e-5
MASKED = -1e30
SCALE = DH ** -0.5

C_IDENT, C_MASK, C_END = 0, 128, 256

OFFSET = {"X": 3, "A": 2, "S": 1, "T": 0, "D": -1, "E": -2}
FIRST_STEP, LOOP_FROM, LOOP_TO, LAST_STEP = -3, 2, 12, 17

SPARE_USES = {
    (0, 1): ("A", "q"),
    (1, 0): ("T", "max1"), (1, 1): ("A", "k"),
    (2, 0): ("D", "sums1"), (2, 1): ("E", "key"),
    (3, 0): ("E", "gate"), (3, 1): ("D", "attnT"),
    (4, 0): ("E", "value"), (4, 1): ("D", "project"),
    (5, 0): ("S", "v"),
    (6, 0): ("S", "max0"),
    (7, 0): ("T", "sums0"),
    (8, 1): ("D", "hT"),
    (9, 0): ("X", "xT"),
}


def is_static(b):
    return isinstance(b, int)


def active(stage, b):
    return not is_static(b) or 0 <= b + OFFSET[stage] < BATCH


def before(stage, b):
    n = b + OFFSET[stage]
    return min(max(n, 0), BATCH) if is_static(b) else n


def spare_before(b, name=None):
    n = 0
    for stage in OFFSET:
        uses = sum(s == stage for s, _ in SPARE_USES.values())
        n = n + uses * before(stage, b)
    for _, (stage, use) in sorted(SPARE_USES.items()):
        if use == name:
            break
        if name is not None and active(stage, b):
            n = n + 1
    return n


def last_use(b, name):
    stage = next(s for s, use in SPARE_USES.values() if use == name)
    return spare_before(b - 1, name) + (1 if active(stage, b - 1) else 0)


def chunk(c, i, blocks):
    full, wide, half, narrow = blocks
    if c == CHUNKS - 1:
        return [(i - i % 2 + j, i % 2, half, SEQ // 2 * j, SEQ // 2) for j in range(2)]
    head = (c // 2 + i) % 2
    if c % 2 == 0:
        return [(i, head, full, 0, SEQ)]
    return [(i, head, wide, 0, SEQ - BLK), (i, head, narrow, SEQ - BLK, BLK)]


def exp_chunk(c, i):
    return chunk(c, i, (0, 1, 2, 3))


def max_chunk(c, i):
    return chunk(c, i, (3, 2, 1, 0))


def block_program(nc, x, W1, b1, Wp, bp, Wr, Wk, Wv, mu_r, mu_k, consts, out):
    with ExitStack() as ctx:
        def sb(name, shape, dt=F32):
            return ctx.enter_context(nc.sbuf_tensor(name, shape, dt))

        def ps(name, shape):
            return ctx.enter_context(nc.psum_tensor(name, shape, F32))

        def sem(name):
            return ctx.enter_context(nc.semaphore(name))

        cst = sb("cst", [P, C_END])
        ident = cst[:, C_IDENT:C_IDENT + P]
        ident16 = sb("ident16", [P, P], BF16)
        qmask = sb("qmask", [BLK, BLK], BF16)
        w1 = sb("w1", [E, 3 * E])
        w1p = sb("w1p", [E, 3, E])
        wff = sb("wff", [E, 3, E])
        wffT = sb("wffT", [E, 3, E])
        wp = sb("wp", [E, E])
        rows = sb("rows", [1, 4 * E])
        rowsp = sb("rowsp", [1, 3, E])
        ones = sb("ones", [1, P])
        bias = sb("bias", [P, 2 * E])
        vcol = sb("vcol", [E, 1])
        mus = sb("mus", [P, 2])
        half_power = sb("half_power", [P, TT])
        xa = sb("xa", [P, TT, E])
        xT = sb("xT", [P, 2, SEQ])
        qk_rest = sb("qk_rest", [P, 2, SEQ])
        qk_parts = sb("qk_parts", [P, 2 * PARTS, SEQ], BF16)
        qop = sb("qop", [P, 2, PAIRS, SEQ], BF16)
        kop = sb("kop", [P, 2, PAIRS, SEQ], BF16)
        vop = sb("vop", [P, 2, TT, PAIRS, 2, 4 * DH])
        rowmax = sb("rowmax", [P, 2, PAIRS * 2 * NBLK])
        negmax = sb("negmax", [MAXIMA, P])
        negmax_parts = sb("negmax_parts", [MAXIMA, MROWS, P], BF16)
        probs = sb("probs", [P, 2, QUARTET, SEQ])
        osum = sb("osum", [P, 2, SEQ])
        inv = sb("inv", [P, 2, TT, QUARTET, 2])
        attn = sb("attn", [P, TT, HEADS, DH])
        attnT = sb("attnT", [E, SEQ])
        xres = sb("xres", [P, TT, E])
        xbias = sb("xbias", [P, TT, E])
        y = sb("y", [P, TT, E])
        stats = sb("stats", [P, 2, TT, 6])
        moments = sb("moments", [P, 2, TT, 2])
        vareps = sb("vareps", [P, 2, TT])
        rstd = sb("rstd", [P, 2, TT])
        shift = sb("shift", [P, 2, TT])
        h = sb("h", [P, 2, TT, E])
        hT = sb("hT", [P, SEQ + 1])
        step_d = sb("step_d", [P, SEQ])
        scaled = sb("scaled", [P, 2, SEQ])
        mixed = sb("mixed", [P, 2, SEQ])
        krelu = sb("krelu", [P, SEQ])
        ksq = sb("ksq", [P, SEQ])
        gate = sb("gate", [P, SEQ])
        gated = sb("gated", [P, SEQ])
        z = sb("z", [P, TT, E])
        result = sb("result", [P, TT, E])

        tps = ps("tps", [P, 2, SEQ])
        sps = ps("sps", [P, 2, 2, SEQ])
        ops = ps("ops", [P, SEQ])
        spare = ps("spare", [P, SEQ])

        d_parts = nc.dram_tensor("d_parts", (2, 2, 2, PAIRS, DH, PARTS, SEQ), BF16, kind="Internal").ap()
        d_max = nc.dram_tensor("d_max", (2, MROWS, MAXIMA, BLK), BF16, kind="Internal").ap()

        weights_in = sem("weights_in")
        kop_cleared = sem("kop_cleared")
        vop_cleared = sem("vop_cleared")
        setup_pe = sem("setup_pe")
        setup_act = sem("setup_act")
        setup_dve = sem("setup_dve")
        armed = sem("armed")
        xa_in = sem("xa_in")
        xres_in = sem("xres_in")
        spare_written = sem("spare_written")
        spare_read = sem("spare_read")
        qk_split = sem("qk_split")
        qk_high = sem("qk_high")
        qk_middle = sem("qk_middle")
        parts_out = sem("parts_out")
        ops_in = [sem("ops_in0"), sem("ops_in1")]
        s_done = sem("s_done")
        s_reduced = sem("s_reduced")
        max_copied = sem("max_copied")
        max_high = sem("max_high")
        max_split = sem("max_split")
        max_out = sem("max_out")
        max_in = [sem("max_in0"), sem("max_in1")]
        t_done = sem("t_done")
        exp_done = sem("exp_done")
        masked = sem("masked")
        pv_done = sem("pv_done")
        o_copied = sem("o_copied")
        inv_done = sem("inv_done")
        xbias_done = sem("xbias_done")
        stats_done = sem("stats_done")
        moments_done = sem("moments_done")
        vareps_done = sem("vareps_done")
        rstd_done = sem("rstd_done")
        shift_done = sem("shift_done")
        h_done = sem("h_done")
        hT_copied = sem("hT_copied")
        step_done = sem("step_done")
        scaled_done = sem("scaled_done")
        mixed_done = sem("mixed_done")
        krelu_done = sem("krelu_done")
        ksq_done = sem("ksq_done")
        z_done = sem("z_done")
        stats2_done = sem("stats2_done")
        moments2_done = sem("moments2_done")
        vareps2_done = sem("vareps2_done")
        rstd2_done = sem("rstd2_done")
        shift2_done = sem("shift2_done")
        result_done = sem("result_done")
        stored = sem("stored")

        def wait(eng, semaphore, value, alone=True):
            if is_static(value):
                if value > 0:
                    eng.wait_ge(semaphore, value)
            else:
                value = eng.to_reg(value)
                if alone:
                    eng.wait_ge(armed, 1)
                eng.wait_ge(semaphore, value)

        def part(i, t):
            return qk_parts[:, t if i == 0 else 2 * PARTS - 1 - t, :]

        def run_steps(eng, step):
            for b in range(FIRST_STEP, LOOP_FROM):
                step(b, b % 2)
            with eng.Fori(LOOP_FROM, LOOP_TO, 2) as b:
                step(b, LOOP_FROM % 2)
                step(b + 1, (LOOP_FROM + 1) % 2)
            for b in range(LOOP_TO, LAST_STEP + 1):
                step(b, b % 2)

        block = ctx.enter_context(nc.Block())

        @block.sync
        def _(sp):
            for dst, src in (
                (cst[:], consts),
                (w1[:], W1),
                (wp[:], Wp),
                (wff[:, 0, :], Wr), (wff[:, 1, :], Wk), (wff[:, 2, :], Wv),
                (rows[:, 0:3 * E], b1.rearrange("(o n) -> o n", o=1)),
                (rows[:, 3 * E:], bp.rearrange("(o n) -> o n", o=1)),
                (mus[:, 0:1], mu_r.rearrange("(n o) -> n o", o=1)),
                (mus[:, 1:2], mu_k.rearrange("(n o) -> n o", o=1)),
            ):
                sp.dma_start(dst, src).then_inc(weights_in, 16)
            def load_operands(par, half):
                prs = slice(QUARTET * half, QUARTET * half + QUARTET)
                for hh in range(2):
                    r = HROWS * hh
                    for qk_i, operand, order in ((0, qop, (0, 0, 1)), (1, kop, (2, 1, 2))):
                        src = d_parts[par, qk_i, hh, prs]
                        for i, part in enumerate(order):
                            sp.dma_start(operand[r + DH * i:r + DH * i + DH, par, prs, :],
                                         src[:, :, part, :].rearrange("p d n -> d p n")).then_inc(ops_in[half], 16)
                        sp.dma_start(operand[r + LEADING:r + TERMS, par, prs, :],
                                     src.rearrange("p d t n -> (d t) p n")).then_inc(ops_in[half], 16)

            def load_max(par, half, count):
                wait(sp, max_split, count + 1)
                sp.dma_start(d_max[half].rearrange("i r q -> r i q"), negmax_parts[:]).then_inc(max_out, 16)
                wait(sp, max_out, 16 * (count + 1))
                for hh in range(2):
                    r = HROWS * hh + TERMS
                    sp.dma_start(qop[r:r + MROWS, par, QUARTET * half:QUARTET * half + QUARTET, :],
                                 d_max[half].rearrange("i (p h a) q -> h i p (a q)", h=2, a=NBLK)[hh])\
                        .then_inc(max_in[half], 16)

            def step(b, par):
                other = 1 - par
                if active("S", b):
                    wait(sp, parts_out, 16 * before("A", b))
                    wait(sp, t_done, 4 * GROUPS * before("T", b))
                    wait(sp, s_done, 2 * GROUPS * before("S", b))
                    load_operands(other, 1)
                if active("T", b):
                    load_max(par, 1, 2 * before("T", b) + 1)
                if active("X", b):
                    wait(sp, spare_written, spare_before(b))
                    sp.dma_start(xa[:], x[b + OFFSET["X"]].rearrange("(t p) e -> p t e", p=P)).then_inc(xa_in, 16)
                if active("D", b):
                    wait(sp, xbias_done, before("D", b))
                    sp.dma_start(xres[:], x[b + OFFSET["D"]].rearrange("(t p) e -> p t e", p=P)).then_inc(xres_in, 16)
                if active("A", b):
                    wait(sp, qk_split, 2 * (before("A", b) + 1))
                    wait(sp, ops_in[0], 256 * before("A", b))
                    wait(sp, ops_in[1], 256 * before("S", b))
                    sp.dma_start(d_parts[par].rearrange("k h p d t n -> (h p d) k t n"),
                                 qk_parts[:].rearrange("r (k t) n -> r k t n", k=2)).then_inc(parts_out, 16)
                if active("A", b):
                    wait(sp, parts_out, 16 * (before("A", b) + 1))
                    if active("T", b):
                        wait(sp, t_done, 4 * GROUPS * before("T", b) + 4 * CHUNKS)
                    if active("S", b):
                        wait(sp, s_done, 2 * GROUPS * before("S", b) + GROUPS)
                    load_operands(par, 0)
                if active("S", b):
                    load_max(other, 0, 2 * before("S", b))
                if active("E", b):
                    wait(sp, result_done, before("E", b) + 1)
                    sp.dma_start(out[b + OFFSET["E"]].rearrange("(t p) e -> p t e", p=P), result[:]).then_inc(stored, 16)

            sp.wait_ge(kop_cleared, 1)
            run_steps(sp, step)
            sp.wait_ge(stored, 16 * BATCH)

        @block.tensor
        def _(pe):
            pe.wait_ge(weights_in, 16 * 10)
            for i in range(3):
                last = nc.tensor.transpose(spare[:, E * i:E * i + E], wff[:, i, :], ident)
            last.then_inc(setup_pe, 1)
            pe.wait_ge(setup_act, 1)
            pe.wait_ge(setup_dve, 1)
            for i in range(3):
                last = nc.tensor.matmul(spare[:, i:i + 1], rowsp[:, i, :], ones[:, 0:1], start=True, stop=True)
            last.then_inc(setup_pe, 1)
            pe.wait_ge(setup_act, 2)
            nc.tensor.matmul(spare[:, E:2 * E], ones[:], rows[:, 3 * E:], start=True, stop=False)
            nc.tensor.matmul(spare[:, E:2 * E], vcol[:].to_broadcast([E, P]), wp[:], start=False, stop=True)\
                .then_inc(setup_pe, 1)
            pe.wait_ge(armed, 1)

            def rowmax_transpose(par, half):
                return nc.tensor.transpose(spare[0:MAXIMA, 0:P], rowmax[:, par, MAXIMA * half:MAXIMA * half + MAXIMA],
                                           ident)

            def tokens_by_weights(tokensT, weights):
                for t in range(TT):
                    last = nc.tensor.matmul(spare[:, P * t:P * t + P], tokensT[:, P * t:P * t + P], weights,
                                            start=True, stop=True)
                return last

            def spare_use(b, par, g, place):
                stage, use = SPARE_USES.get((g, place), (None, None))
                if stage is None or not active(stage, b):
                    return
                wait(pe, spare_read, spare_before(b, use))
                if use == "xT":
                    wait(pe, xa_in, 16 * (before("X", b) + 1))
                    for t in range(TT):
                        last = nc.tensor.transpose(spare[:, P * t:P * t + P], xa[:, t, :], ident)
                elif use in ("q", "k"):
                    last = nc.tensor.matmul(spare[:], w1p[:, "qk".index(use), :], xT[:, par], start=True, stop=True)
                elif use == "v":
                    last = tokens_by_weights(xT[:, 1 - par], w1p[:, 2, :])
                elif use == "max0":
                    wait(pe, s_reduced, 2 * GROUPS * before("S", b) + GROUPS)
                    last = rowmax_transpose(1 - par, 0)
                elif use == "max1":
                    wait(pe, s_reduced, 2 * GROUPS * (before("T", b) + 1))
                    last = rowmax_transpose(par, 1)
                elif use in ("sums0", "sums1"):
                    half = int(use[-1])
                    wait(pe, o_copied, 2 * before(stage, b) + half + 1)
                    for t in range(TT):
                        last = nc.tensor.transpose(spare[:, P * t:P * t + P], osum[:, half, P * t:P * t + P], ident)
                elif use == "attnT":
                    for t in range(TT):
                        last = nc.tensor.transpose(spare[:, P * t:P * t + P],
                                                   attn[:, t].rearrange("q h d -> q (h d)"), ident)
                elif use == "project":
                    last = tokens_by_weights(attnT, wp[:])
                elif use == "hT":
                    wait(pe, h_done, before("D", b) + 1)
                    for t in range(TT):
                        last = nc.tensor.transpose(spare[:, P * t:P * t + P], h[:, 1 - par, t, :], ident)
                elif use == "key":
                    wait(pe, mixed_done, 2 * (before("E", b) + 1))
                    last = nc.tensor.matmul(spare[:], wffT[:, 1, :], mixed[:, 1, :], start=True, stop=True)
                elif use == "gate":
                    last = tokens_by_weights(mixed[:, 0], wffT[:, 0, :])
                elif use == "value":
                    wait(pe, ksq_done, before("E", b) + 1)
                    last = tokens_by_weights(ksq, wffT[:, 2, :])
                last.then_inc(spare_written, 1)

            def t_chunk(b, par, g, i):
                n = 4 * GROUPS * before("T", b) + 4 * g + i
                half, c = divmod(g, CHUNKS)
                if c == 0 and i == 0:
                    wait(pe, max_in[half], 32 * (before("T", b) + 1))
                wait(pe, exp_done, n - 1)
                for t, hh, a, off, w in exp_chunk(c, i):
                    pair = QUARTET * half + t
                    r = slice(HROWS * hh, HROWS * hh + TERMS + MROWS)
                    last = nc.tensor.matmul(tps[:, i % 2, off:off + w], kop[r, par, pair, BLK * a:BLK * a + BLK],
                                            qop[r, par, pair, BLK * a:SEQ], start=True, stop=True)
                last.then_inc(t_done, 1)

            def s_chunk(b, par, g, i):
                n = 2 * GROUPS * before("S", b) + 2 * g + i
                half, c = divmod(g, CHUNKS)
                if c == 0 and i == 0:
                    wait(pe, ops_in[half], 256 * (before("S", b) + 1))
                wait(pe, s_reduced, n - 1)
                banks = [max_chunk(c, 2 * i + k) for k in range(2)]
                blocks = len(banks[0])
                for j in range(blocks):
                    for k in range(2):
                        t, hh, a, off, w = banks[k][j]
                        r = slice(HROWS * hh, HROWS * hh + TERMS)
                        pair = QUARTET * half + t
                        nc.tensor.matmul(sps[:, i, k, off:off + w], qop[r, par, pair, BLK * a:BLK * a + BLK],
                                         kop[r, par, pair, 0:w], start=j == 0, stop=False, skip_group_check=True)
                for k in range(2):
                    for j, (_, _, _, off, w) in enumerate(banks[k]):
                        last = nc.tensor.matmul(sps[:, i, k, off + w - BLK:off + w], ident16[:], qmask[:],
                                                start=False, stop=j == blocks - 1, skip_group_check=True)
                last.then_inc(s_done, 1)

            def pv(b, entries, par, g):
                half, c = divmod(g, CHUNKS)
                if c == 0:
                    wait(pe, o_copied, 2 * entries + half)
                    if half == 0:
                        wait(pe, spare_read, last_use(b, "v"))
                wait(pe, masked, GROUPS * entries + g + 1)
                by_pair = sorted((t, hh, j, i) for i in range(QUARTET)
                                 for j, (t, hh, _, _, _) in enumerate(exp_chunk(c, i)))
                per_pair = len(by_pair) // QUARTET
                for k in range(per_pair):
                    for t in range(QUARTET):
                        _, hh, j, i = by_pair[per_pair * t + k]
                        _, _, a, off, w = exp_chunk(c, i)[j]
                        last = nc.tensor.matmul(ops[32 * t:32 * t + 32, BLK * a:SEQ],
                                                vop[:, par, a, QUARTET * half + t, hh, :],
                                                probs[:, g % 2, i, off:off + w],
                                                start=c == 0, stop=c == CHUNKS - 1, skip_group_check=True)
                last.then_inc(pv_done, 1)

            def step(b, par):
                for g in range(GROUPS):
                    if active("T", b):
                        t_chunk(b, par, g, 0)
                        t_chunk(b, par, g, 1)
                    spare_use(b, par, g, 0)
                    if active("S", b):
                        s_chunk(b, 1 - par, g, 0)
                    if active("T", b):
                        t_chunk(b, par, g, 2)
                        t_chunk(b, par, g, 3)
                    spare_use(b, par, g, 1)
                    if active("S", b):
                        s_chunk(b, 1 - par, g, 1)
                    if g == 0 and active("D", b):
                        pv(b, before("D", b), 1 - par, GROUPS - 1)
                    elif g > 0 and active("T", b):
                        pv(b, before("T", b), par, g - 1)

            run_steps(pe, step)

        @block.scalar
        def _(act):
            act.wait_ge(setup_pe, 1)
            nc.scalar.copy(wffT[:, 0:2].rearrange("p a b -> p (a b)"), spare[:, 0:2 * E])
            nc.scalar.activation(wffT[:, 2, :], spare[:, 2 * E:3 * E], ACT.Copy, scale=0.5).then_inc(setup_act, 1)
            act.wait_ge(setup_pe, 2)
            nc.scalar.copy(bias[:, 0:2], spare[:, 0:2])
            nc.scalar.copy(vcol[:], spare[:, 2:3]).then_inc(setup_act, 1)
            act.wait_ge(setup_pe, 3)
            nc.scalar.copy(bias[:, E:2 * E], spare[:, E:2 * E]).then_inc(setup_act, 1)
            act.wait_ge(setup_act, 3)
            act.wait_ge(armed, 1)

            def spare_use(b, par, g, place):
                stage, use = SPARE_USES.get((g, place), (None, None))
                if stage is None or not active(stage, b) or use in ("sums0", "sums1", "project", "value"):
                    return
                n = before(stage, b)
                if use in ("max0", "max1"):
                    m = 2 * n + (0 if use == "max0" else 1)
                    wait(act, max_split, m)
                wait(act, spare_written, spare_before(b, use) + 1)
                if use == "xT":
                    ins = nc.scalar.copy(xT[:, 1 - par], spare[:])
                elif use == "v":
                    wait(act, pv_done, GROUPS * before("T", b))
                    for hh in range(2):
                        ins = nc.scalar.copy(vop[:, 1 - par, :, :, hh, DH * hh:DH * hh + DH],
                                             spare[:].rearrange("k (t p h d) -> k h t p d", t=TT, p=PAIRS, h=2)[:, hh])
                elif use == "attnT":
                    ins = nc.scalar.copy(attnT[:], spare[:])
                elif use in ("q", "k"):
                    i = "qk".index(use)
                    wait(act, parts_out, 16 * n)
                    nc.scalar.activation(part(i, 0), spare[:], ACT.Identity, bias=bias[:, i:i + 1])\
                        .then_inc(qk_high, 1)
                    return
                elif use in ("max0", "max1"):
                    ins = nc.scalar.activation(negmax[:], spare[0:MAXIMA, 0:P], ACT.Copy, scale=-1.0)
                elif use == "hT":
                    wait(act, mixed_done, 2 * n)
                    ins = nc.scalar.copy(hT[:, 1:SEQ + 1], spare[:])
                elif use == "key":
                    wait(act, ksq_done, n)
                    ins = nc.scalar.activation(krelu[:], spare[:], ACT.Relu)
                elif use == "gate":
                    ins = nc.scalar.activation(gate[:], spare[:], ACT.Tanh, scale=0.5)
                ins.then_inc(spare_read, 1)

            def exp_chunk_of(b, g, i):
                n = before("T", b)
                half, c = divmod(g, CHUNKS)
                if i == 0:
                    wait(act, pv_done, GROUPS * n + g - 1)
                wait(act, t_done, 4 * GROUPS * n + 4 * g + i + 1)
                nc.scalar.activation(probs[:, g % 2, i, :], tps[:, i % 2, :], ACT.Exp, scale=SCALE)\
                    .then_inc(exp_done, 1)

            def copy_o(n, half, taken):
                wait(act, spare_written, taken)
                wait(act, pv_done, GROUPS * n + CHUNKS * (half + 1))
                nc.scalar.copy(osum[:, half, :], ops[:]).then_inc(o_copied, 1)

            def split_middle(b, i):
                n = 2 * before("A", b) + i
                wait(act, spare_read, spare_before(b, "qk"[i]) + 1)
                nc.scalar.copy(part(i, 1), qk_rest[:, i, :]).then_inc(qk_middle, 1)

            def normalise(i, n, src, dst, done_shift, done):
                wait(act, done_shift, n + 1)
                for t in range(TT):
                    last = nc.scalar.activation(dst[:, t, :], src[:, t, :], ACT.Identity,
                                                bias=shift[:, i, t:t + 1], scale=rstd[:, i, t:t + 1])
                last.then_inc(done, 1)

            def scale_steps(n):
                wait(act, step_done, n + 1)
                wait(act, mixed_done, 2 * n)
                for i in range(2):
                    nc.scalar.activation(scaled[:, i, :], step_d[:], ACT.Copy, scale=mus[:, i:i + 1])\
                        .then_inc(scaled_done, 1)

            def step(b, par):
                for g in range(GROUPS):
                    if active("T", b):
                        exp_chunk_of(b, g, 0)
                        exp_chunk_of(b, g, 1)
                    spare_use(b, par, g, 0)
                    if g == 1 and active("D", b):
                        copy_o(before("D", b), 1, last_use(b, "sums1"))
                    if g == CHUNKS + 1 and active("T", b):
                        copy_o(before("T", b), 0, last_use(b, "sums0"))
                    if active("T", b):
                        exp_chunk_of(b, g, 2)
                        exp_chunk_of(b, g, 3)
                    spare_use(b, par, g, 1)
                    if g in (1, 2) and active("A", b):
                        split_middle(b, g - 1)
                    if g == 7 and active("D", b):
                        wait(act, z_done, before("E", b))
                        normalise(0, before("D", b), y, h[:, 1 - par], shift_done, h_done)
                    if g == 8 and active("E", b):
                        n = before("E", b)
                        wait(act, stored, 16 * n)
                        normalise(1, n, z, result, shift2_done, result_done)
                    if g == 9 and active("D", b):
                        scale_steps(before("D", b))

            run_steps(act, step)

        @block.vector
        def _(dve):
            nc.vector.memset(ones[:], 1.0)
            nc.vector.memset(kop[:], 1.0).then_inc(kop_cleared, 1)
            nc.vector.memset(hT[:, 0:1], 0.0)
            dve.wait_ge(vop_cleared, 1)
            for hh in range(2):
                last = nc.vector.memset(vop[:].rearrange("k b t p h c -> k (b t p) h c")[
                    :, :, hh, (2 + hh) * DH:(3 + hh) * DH], 1.0)
            last.then_inc(vop_cleared, 1)
            dve.wait_ge(weights_in, 16 * 10)
            nc.vector.tensor_copy(ident16[:], ident)
            nc.vector.tensor_copy(qmask[:], cst[:, C_MASK:C_MASK + BLK])
            for i in range(3):
                order = "c (h p d) -> c h p d" if i < 2 else "c (p h d) -> c h p d"
                nc.vector.tensor_copy(
                    w1p[:, i, :].rearrange(order, h=2, d=DH),
                    w1[:].rearrange("c (p h i d) -> c i h p d", h=2, i=3, d=DH)[:, i])
                last = nc.vector.tensor_copy(
                    rowsp[:, i, :].rearrange(order, h=2, d=DH),
                    rows[:, 0:3 * E].rearrange("c (p h i d) -> c i h p d", h=2, i=3, d=DH)[:, i])
            last.then_inc(setup_dve, 1)
            dve.wait_ge(setup_dve, 1)
            dve.wait_ge(setup_act, 3)
            nc.vector.memset(half_power[:], -0.5).then_inc(armed, 1)

            def reduce_chunk(b, par, g, i):
                n = 2 * GROUPS * before("S", b) + 2 * g + i
                half, c = divmod(g, CHUNKS)
                wait(dve, s_done, n + 1, alone=False)
                for j in range(len(max_chunk(c, 0))):
                    (t0, h0, a, off, w), (t1, h1, _, _, _) = (max_chunk(c, 2 * i + k)[j] for k in range(2))
                    first, second = (((QUARTET * half + t) * 2 + hh) * NBLK + a for t, hh in ((t0, h0), (t1, h1)))
                    last = nc.vector.reduce_max(rowmax[:, par, first:second + 1:second - first],
                                                sps[:, i, :, off:off + w], axis=AX_X)
                last.then_inc(s_reduced, 1)

            def layer_norm_moments(src, i, n, ready, value, done_stats, done_moments):
                wait(dve, ready, value)
                for t in range(TT):
                    last = nc.vector.bn_stats(out=stats[:, i, t, :], in_=src[:, t, :])
                last.then_inc(done_stats, 1)
                wait(dve, done_stats, n + 1)
                for t in range(TT):
                    last = nc.vector.bn_aggr(out=moments[:, i, t, :], in_=stats[:, i, t, :])
                last.then_inc(done_moments, 1)

            def spare_use(b, par, g, place):
                stage, use = SPARE_USES.get((g, place), (None, None))
                if stage is None or not active(stage, b):
                    return
                n = before(stage, b)
                written = spare_before(b, use) + 1
                if use in ("q", "k"):
                    i = "qk".index(use)
                    wait(dve, qk_high, 2 * n + i + 1)
                    wait(dve, qk_split, 2 * (n - 1) + i + 1)
                    nc.vector.scalar_tensor_tensor(qk_rest[:, i, :], spare[:], bias[:, i:i + 1], part(i, 0),
                                                   ALU.add, ALU.subtract).then_inc(spare_read, 1)
                elif use in ("sums0", "sums1"):
                    half = int(use[-1])
                    wait(dve, spare_written, written)
                    tiles = spare[:].rearrange("q (t r s h d) -> q s t r h d", t=TT, r=QUARTET, s=2, h=2)
                    nc.vector.reciprocal(inv[:, half], tiles[:, 1, :, :, :, 0]).then_inc(inv_done, 1)
                    wait(dve, inv_done, 2 * n + half + 1)
                    for t in range(TT):
                        last = nc.vector.tensor_tensor(
                            attn[:, t, DH * half:DH * half + DH].rearrange("q (r h) d -> q r h d", h=2),
                            tiles[:, 0, t], inv[:, half, t].unsqueeze(3).to_broadcast([P, QUARTET, 2, DH]), ALU.mult)
                    last.then_inc(spare_read, 1)
                elif use == "project":
                    wait(dve, xbias_done, n + 1)
                    wait(dve, h_done, n)
                    wait(dve, spare_written, written)
                    nc.vector.tensor_tensor(y[:].rearrange("p t e -> p (t e)"), spare[:],
                                            xbias[:].rearrange("p t e -> p (t e)"), ALU.add).then_inc(spare_read, 1)
                elif use == "value":
                    wait(dve, z_done, n)
                    wait(dve, spare_written, written)
                    nc.vector.scalar_tensor_tensor(gated[:], gate[:], 1.0, spare[:], ALU.add, ALU.mult)\
                        .then_inc(spare_read, 1)

            def shift_by_mean(i, n, done_rstd, done):
                wait(dve, done_rstd, n + 1)
                nc.vector.scalar_tensor_tensor(shift[:, i, :], moments[:, i, :, 0], -1.0, rstd[:, i, :],
                                               ALU.mult, ALU.mult).then_inc(done, 1)

            def step(b, par):
                for g in range(GROUPS):
                    spare_use(b, par, g, 0)
                    if active("S", b):
                        reduce_chunk(b, 1 - par, g, 0)
                    if g == 5 and active("D", b):
                        layer_norm_moments(y, 0, before("D", b), spare_read, spare_before(b, "project") + 1,
                                           stats_done, moments_done)
                    if g == 6 and active("E", b):
                        layer_norm_moments(z, 1, before("E", b), z_done, before("E", b) + 1, stats2_done, moments2_done)
                    spare_use(b, par, g, 1)
                    if active("S", b):
                        reduce_chunk(b, 1 - par, g, 1)
                    if g == 6 and active("D", b):
                        shift_by_mean(0, before("D", b), rstd_done, shift_done)
                    if g == 7 and active("E", b):
                        shift_by_mean(1, before("E", b), rstd2_done, shift2_done)

            run_steps(dve, step)

        @block.gpsimd
        def _(pool):
            nc.gpsimd.memset(vop[:], 0.0).then_inc(vop_cleared, 1)
            pool.wait_ge(armed, 1)

            def mask_group(b, g):
                n = before("T", b)
                wait(pool, exp_done, 4 * GROUPS * n + 4 * g + 4)
                for _, _, _, off, _ in exp_chunk(g % CHUNKS, 0):
                    v = probs[:, g % 2, :, off:off + BLK]
                    last = nc.gpsimd.affine_select(out=v, in_=v, compare_op=ALU.is_ge, fill=0.0, base=0,
                                                   pattern=[[0, QUARTET], [1, BLK]], channel_multiplier=-1)
                last.then_inc(masked, 1)

            def split_low(b, i):
                wait(pool, qk_middle, 2 * before("A", b) + i + 1)
                nc.gpsimd.tensor_tensor(part(i, 2), qk_rest[:, i, :], part(i, 1), ALU.subtract).then_inc(qk_split, 1)

            def split_max(n, b, use):
                wait(pool, spare_read, spare_before(b, use) + 1)
                wait(pool, max_out, 16 * n)
                nc.gpsimd.tensor_scalar(negmax_parts[:, 0, :], negmax[:], 1.0, 0.0, ALU.mult, ALU.add).then_inc(max_high, 1)
                wait(pool, max_high, n + 1)
                nc.gpsimd.tensor_tensor(negmax_parts[:, 1, :], negmax[:], negmax_parts[:, 0, :], ALU.subtract)\
                    .then_inc(max_split, 1)

            def inverse_deviation(i, n, done_moments, done_eps, done_rstd):
                wait(pool, done_moments, n + 1)
                nc.gpsimd.tensor_scalar(vareps[:, i, :], moments[:, i, :, 1], EPS, None, ALU.add).then_inc(done_eps, 1)
                wait(pool, done_eps, n + 1)
                nc.gpsimd.tensor_tensor(rstd[:, i, :], vareps[:, i, :], half_power[:], ALU.pow).then_inc(done_rstd, 1)

            def mix_step(n, b):
                wait(pool, spare_read, spare_before(b, "hT") + 1)
                nc.gpsimd.tensor_tensor(step_d[:], hT[:, 1:SEQ + 1], hT[:, 0:SEQ], ALU.subtract).then_inc(step_done, 1)

            def mix_sum(n):
                for i in range(2):
                    wait(pool, scaled_done, 2 * n + i + 1)
                    nc.gpsimd.tensor_tensor(mixed[:, i, :], scaled[:, i, :], hT[:, 0:SEQ], ALU.add)\
                        .then_inc(mixed_done, 1)

            def step(b, par):
                for g in range(GROUPS):
                    if g == 0 and active("E", b):
                        mix_sum(before("E", b))
                    if g == 3 and active("E", b):
                        wait(pool, spare_read, spare_before(b, "key") + 1)
                        nc.gpsimd.tensor_tensor(ksq[:], krelu[:], krelu[:], ALU.mult).then_inc(ksq_done, 1)
                    if g == 2 and active("T", b):
                        split_max(2 * before("T", b) + 1, b, "max1")
                    if g in (2, 3) and active("A", b):
                        split_low(b, g - 2)
                    if g == 3 and active("D", b):
                        n = before("D", b)
                        wait(pool, xres_in, 16 * (n + 1))
                        wait(pool, h_done, n)
                        nc.gpsimd.tensor_tensor(xbias[:], xres[:],
                                                bias[:, E:2 * E].unsqueeze(1).to_broadcast([P, TT, E]),
                                                ALU.add).then_inc(xbias_done, 1)
                    if g == 5 and active("E", b):
                        n = before("E", b)
                        wait(pool, spare_read, spare_before(b, "value") + 1)
                        wait(pool, result_done, n)
                        nc.gpsimd.tensor_tensor(z[:].rearrange("p t e -> p (t e)"), gated[:],
                                                h[:, par].rearrange("p t e -> p (t e)"), ALU.add).then_inc(z_done, 1)
                    if g == 6 and active("D", b):
                        inverse_deviation(0, before("D", b), moments_done, vareps_done, rstd_done)
                    if g == 7 and active("E", b):
                        inverse_deviation(1, before("E", b), moments2_done, vareps2_done, rstd2_done)
                    if g == 7 and active("S", b):
                        split_max(2 * before("S", b), b, "max0")
                    if g == 9 and active("D", b):
                        mix_step(before("D", b), b)
                    if active("T", b):
                        mask_group(b, g)

            run_steps(pool, step)


def shape_constants(np):
    c = np.zeros((P, C_END), np.float32)
    c[:, C_IDENT:C_IDENT + P] = np.eye(P)
    c[:, C_MASK:C_MASK + BLK] = np.triu(np.full((BLK, BLK), MASKED), 1)
    return c


INPUTS = ["L0_attn_x", "L0_attn_W1", "L0_attn_b1", "L0_attn_Wp", "L0_attn_bp",
          "L0_ffn_W_r", "L0_ffn_W_k", "L0_ffn_W_v", "L0_ffn_mu_r", "L0_ffn_mu_k"]


def kernel(**inputs):
    import numpy as np
    import concourse.bacc as bacc
    from concourse.bass_utils import run_bass_kernel_spmd

    nc = bacc.Bacc("TRN2", target_bir_lowering=False, num_devices=1)
    arrays = {name: np.ascontiguousarray(inputs[name]) for name in INPUTS}
    arrays["shape_constants"] = shape_constants(np)
    args = [nc.dram_tensor(name, a.shape, mybir.dt.from_np(a.dtype), kind="ExternalInput").ap()
            for name, a in arrays.items()]
    args.append(nc.dram_tensor("out", (BATCH, SEQ, E), F32, kind="ExternalOutput").ap())
    block_program(nc, *args)
    return run_bass_kernel_spmd(nc, [arrays], core_ids=[0]).results[0]["out"]
```

```python
from contextlib import ExitStack

import concourse.bass as bass
from concourse import mybir

F32 = mybir.dt.float32
BF16 = mybir.dt.bfloat16
ACT = mybir.ActivationFunctionType
ALU = mybir.AluOpType
AX_X = mybir.AxisListType.X

P = 128
BATCH, SEQ, E = 16, 512, 128
HEADS, DH = 16, 8
PAIRS = HEADS // 2
BLK = 128
HROWS = 64
QBLK = 64
NQBLK = SEQ // QBLK
TT = SEQ // P
CHUNKS = 5
GROUPS = 2 * CHUNKS
BANKS = 3
QUARTET = 4
TERMS = 6 * DH
MROWS = 2
LEADING = 3 * DH
MAXIMA = QUARTET * NQBLK
PARTS = 3
LOADED = 16 * 2 * 2 * 4
EPS = 1e-5
MASKED = -1e30
SCALE = DH ** -0.5

C_IDENT, C_DUP, C_MASK, C_END = 0, 128, 256, 320

OFFSET = {"X": 3, "A": 2, "S": 1, "T": 0, "D": -1, "E": -2}
FIRST_STEP, LOOP_FROM, LOOP_TO, LAST_STEP = -3, 2, 12, 17

SPARE_USES = {
    (0, 1): ("A", "q"),
    (1, 0): ("T", "max1"), (1, 1): ("A", "k"),
    (2, 0): ("E", "key"), (2, 1): ("D", "sums1"),
    (3, 0): ("E", "gate"), (3, 1): ("D", "attnT"),
    (4, 1): ("E", "value"),
    (5, 0): ("D", "project"), (5, 1): ("S", "v"),
    (6, 0): ("S", "max0"), (6, 1): ("X", "xT"),
    (8, 0): ("D", "hT"),
    (8, 1): ("T", "sums0"),
}


def bank(m):
    last = QUARTET * GROUPS - 1
    return 1 if m == last else m % BANKS


def bank_free(n, m):
    steps_back = next(d for d in range(1, QUARTET * GROUPS)
                      if bank((m - d) % (QUARTET * GROUPS)) == bank(m))
    return n - steps_back + 1


def is_static(b):
    return isinstance(b, int)


def active(stage, b):
    return not is_static(b) or 0 <= b + OFFSET[stage] < BATCH


def before(stage, b):
    n = b + OFFSET[stage]
    return min(max(n, 0), BATCH) if is_static(b) else n


def spare_before(b, name=None):
    n = 0
    for stage in OFFSET:
        uses = sum(s == stage for s, _ in SPARE_USES.values())
        n = n + uses * before(stage, b)
    for _, (stage, use) in sorted(SPARE_USES.items()):
        if use == name:
            break
        if name is not None and active(stage, b):
            n = n + 1
    return n


def last_use(b, name):
    stage = next(s for s, use in SPARE_USES.values() if use == name)
    return spare_before(b - 1, name) + (1 if active(stage, b - 1) else 0)


def exp_chunk(c, i):
    if c == CHUNKS - 1:
        return [(i - i % 2 + j, i % 2, 2, SEQ // 2 * j, SEQ // 2) for j in range(2)]
    head = (c // 2 + i) % 2
    if c % 2 == 0:
        return [(i, head, 0, 0, SEQ)]
    return [(i, head, 1, 0, SEQ - BLK), (i, head, 3, SEQ - BLK, BLK)]


def max_chunk(c):
    wide = SEQ - QBLK * c
    if c in (0, CHUNKS - 1):
        return [(NQBLK - 1 - c, 0, wide)]
    return [(NQBLK - 1 - c, 0, wide), (c - 1, wide, SEQ - wide)]


def block_program(nc, x, W1, b1, Wp, bp, Wr, Wk, Wv, mu_r, mu_k, consts, out):
    with ExitStack() as ctx:
        def sb(name, shape, dt=F32):
            return ctx.enter_context(nc.sbuf_tensor(name, shape, dt))

        def ps(name, shape):
            return ctx.enter_context(nc.psum_tensor(name, shape, F32))

        def sem(name):
            return ctx.enter_context(nc.semaphore(name))

        cst = sb("cst", [P, C_END])
        ident = cst[:, C_IDENT:C_IDENT + P]
        dup = sb("dup", [QBLK, P], BF16)
        qmask = sb("qmask", [QBLK, QBLK], BF16)
        w1 = sb("w1", [E, 3 * E])
        w1p = sb("w1p", [E, 3, E])
        wff = sb("wff", [E, 3, E])
        wffT = sb("wffT", [E, 3, E])
        wp = sb("wp", [E, E])
        rows = sb("rows", [1, 4 * E])
        rowsp = sb("rowsp", [1, 3, E])
        ones = sb("ones", [1, P])
        bias = sb("bias", [P, 2 * E])
        vcol = sb("vcol", [E, 1])
        mus = sb("mus", [P, 2])
        half_power = sb("half_power", [P, TT])
        xa = sb("xa", [P, TT, E])
        xT = sb("xT", [P, 2, SEQ])
        qk_rest = sb("qk_rest", [P, 2, SEQ])
        qk_parts = sb("qk_parts", [P, 2 * PARTS, SEQ], BF16)
        qop = sb("qop", [P, 2, PAIRS, SEQ], BF16)
        kop = sb("kop", [P, 2, PAIRS, SEQ], BF16)
        vop = sb("vop", [P, 2, TT, PAIRS, 2, 4 * DH])
        rowmax = sb("rowmax", [P, 2, PAIRS, NQBLK])
        negmax = sb("negmax", [MAXIMA, P])
        negmax_parts = sb("negmax_parts", [MAXIMA, MROWS, P], BF16)
        probs = sb("probs", [P, 2, QUARTET, SEQ])
        osum = sb("osum", [P, 2, SEQ])
        inv = sb("inv", [P, 2, TT, QUARTET, 2])
        attn = sb("attn", [P, TT, HEADS, DH])
        attnT = sb("attnT", [E, SEQ])
        xres = sb("xres", [P, TT, E])
        xbias = sb("xbias", [P, TT, E])
        y = sb("y", [P, TT, E])
        stats = sb("stats", [P, 2, TT, 6])
        moments = sb("moments", [P, 2, TT, 2])
        vareps = sb("vareps", [P, 2, TT])
        rstd = sb("rstd", [P, 2, TT])
        h = sb("h", [P, 2, TT, E])
        hT = sb("hT", [P, SEQ + 1])
        step_d = sb("step_d", [P, SEQ])
        scaled = sb("scaled", [P, 2, SEQ])
        mixed = sb("mixed", [P, 2, SEQ])
        krelu = sb("krelu", [P, SEQ])
        ksq = sb("ksq", [P, SEQ])
        gate = sb("gate", [P, SEQ])
        gated = sb("gated", [P, SEQ])
        z = sb("z", [P, TT, E])
        result = sb("result", [P, TT, E])

        tps = ps("tps", [P, BANKS, SEQ])
        sps = ps("sps", [P, BANKS, SEQ])
        ops = ps("ops", [P, SEQ])
        spare = ps("spare", [P, SEQ])

        d_parts = nc.dram_tensor("d_parts", (2, 2, 2, PAIRS, DH, PARTS, SEQ), BF16, kind="Internal").ap()
        d_max = nc.dram_tensor("d_max", (2, MROWS, 2, MAXIMA, QBLK), BF16, kind="Internal").ap()

        weights_in = sem("weights_in")
        kop_cleared = sem("kop_cleared")
        vop_cleared = sem("vop_cleared")
        setup_pe = sem("setup_pe")
        setup_act = sem("setup_act")
        setup_dve = sem("setup_dve")
        armed = sem("armed")
        xa_in = sem("xa_in")
        xres_in = sem("xres_in")
        spare_written = sem("spare_written")
        spare_read = sem("spare_read")
        qk_split = sem("qk_split")
        qk_high = sem("qk_high")
        qk_middle = sem("qk_middle")
        parts_out = sem("parts_out")
        ops_in = [sem("ops_in0"), sem("ops_in1")]
        s_done = sem("s_done")
        s_reduced = sem("s_reduced")
        max_high = sem("max_high")
        max_split = sem("max_split")
        max_out = sem("max_out")
        max_in = [sem("max_in0"), sem("max_in1")]
        t_done = sem("t_done")
        exp_done = sem("exp_done")
        masked = sem("masked")
        pv_done = sem("pv_done")
        o_copied = sem("o_copied")
        inv_done = sem("inv_done")
        xbias_done = sem("xbias_done")
        stats_done = sem("stats_done")
        moments_done = sem("moments_done")
        vareps_done = sem("vareps_done")
        rstd_done = sem("rstd_done")
        h_done = sem("h_done")
        step_done = sem("step_done")
        scaled_done = sem("scaled_done")
        mixed_done = sem("mixed_done")
        ksq_done = sem("ksq_done")
        z_done = sem("z_done")
        stats2_done = sem("stats2_done")
        moments2_done = sem("moments2_done")
        vareps2_done = sem("vareps2_done")
        rstd2_done = sem("rstd2_done")
        result_done = sem("result_done")
        stored = sem("stored")

        def wait(eng, semaphore, value, alone=True):
            if is_static(value):
                if value > 0:
                    eng.wait_ge(semaphore, value)
            else:
                value = eng.to_reg(value)
                if alone:
                    eng.wait_ge(armed, 1)
                eng.wait_ge(semaphore, value)

        def part(i, t):
            return qk_parts[:, t if i == 0 else 2 * PARTS - 1 - t, :]

        def run_steps(eng, step):
            for b in range(FIRST_STEP, LOOP_FROM):
                step(b, b % 2)
            with eng.Fori(LOOP_FROM, LOOP_TO, 2) as b:
                step(b, LOOP_FROM % 2)
                step(b + 1, (LOOP_FROM + 1) % 2)
            for b in range(LOOP_TO, LAST_STEP + 1):
                step(b, b % 2)

        block = ctx.enter_context(nc.Block())

        @block.sync
        def _(sp):
            for dst, src in (
                (cst[:], consts),
                (w1[:], W1),
                (wp[:], Wp),
                (wff[:, 0, :], Wr), (wff[:, 1, :], Wk), (wff[:, 2, :], Wv),
                (rows[:, 0:3 * E], b1.rearrange("(o n) -> o n", o=1)),
                (rows[:, 3 * E:], bp.rearrange("(o n) -> o n", o=1)),
                (mus[:, 0:1], mu_r.rearrange("(n o) -> n o", o=1)),
                (mus[:, 1:2], mu_k.rearrange("(n o) -> n o", o=1)),
            ):
                sp.dma_start(dst, src).then_inc(weights_in, 16)
            def load_operands(par, half):
                prs = slice(QUARTET * half, QUARTET * half + QUARTET)
                for hh in range(2):
                    r = HROWS * hh
                    for qk_i, operand, order in ((0, qop, (0, 0, 1)), (1, kop, (2, 1, 2))):
                        src = d_parts[par, qk_i, hh, prs]
                        for i, part in enumerate(order):
                            sp.dma_start(operand[r + DH * i:r + DH * i + DH, par, prs, :],
                                         src[:, :, part, :].rearrange("p d n -> d p n")).then_inc(ops_in[half], 16)
                        sp.dma_start(operand[r + LEADING:r + TERMS, par, prs, :],
                                     src.rearrange("p d t n -> (d t) p n")).then_inc(ops_in[half], 16)

            def load_max(par, half, count):
                wait(sp, max_split, count + 1)
                sp.dma_start(d_max[half].rearrange("i h r q -> r i h q"),
                             negmax_parts[:].rearrange("r i (h q) -> r i h q", h=2)).then_inc(max_out, 16)
                wait(sp, max_out, 16 * (count + 1))
                for hh in range(2):
                    r = HROWS * hh + TERMS
                    sp.dma_start(qop[r:r + MROWS, par, QUARTET * half:QUARTET * half + QUARTET, :],
                                 d_max[half, :, hh].rearrange("i (p a) q -> i p (a q)", a=NQBLK))\
                        .then_inc(max_in[half], 16)

            def step(b, par):
                other = 1 - par
                if active("S", b):
                    wait(sp, parts_out, 16 * before("A", b))
                    wait(sp, t_done, 4 * GROUPS * before("T", b))
                    wait(sp, s_done, 4 * GROUPS * before("S", b))
                    load_operands(other, 1)
                if active("T", b):
                    load_max(par, 1, 2 * before("T", b) + 1)
                if active("X", b):
                    wait(sp, spare_written, spare_before(b))
                    sp.dma_start(xa[:], x[b + OFFSET["X"]].rearrange("(t p) e -> p t e", p=P)).then_inc(xa_in, 16)
                if active("D", b):
                    wait(sp, xbias_done, before("D", b))
                    sp.dma_start(xres[:], x[b + OFFSET["D"]].rearrange("(t p) e -> p t e", p=P)).then_inc(xres_in, 16)
                if active("A", b):
                    wait(sp, qk_split, 2 * (before("A", b) + 1))
                    wait(sp, ops_in[0], LOADED * before("A", b))
                    wait(sp, ops_in[1], LOADED * before("S", b))
                    sp.dma_start(d_parts[par].rearrange("k h p d t n -> (h p d) k t n"),
                                 qk_parts[:].rearrange("r (k t) n -> r k t n", k=2)).then_inc(parts_out, 16)
                if active("A", b):
                    wait(sp, parts_out, 16 * (before("A", b) + 1))
                    if is_static(b) and before("A", b) == 0:
                        sp.wait_ge(kop_cleared, 1)
                    if active("T", b):
                        wait(sp, t_done, 4 * GROUPS * before("T", b) + 4 * CHUNKS)
                    if active("S", b):
                        wait(sp, s_done, 4 * GROUPS * before("S", b) + 2 * GROUPS)
                    load_operands(par, 0)
                if active("S", b):
                    load_max(other, 0, 2 * before("S", b))
                if active("E", b):
                    wait(sp, result_done, before("E", b) + 1)
                    sp.dma_start(out[b + OFFSET["E"]].rearrange("(t p) e -> p t e", p=P), result[:]).then_inc(stored, 16)

            run_steps(sp, step)
            sp.wait_ge(stored, 16 * BATCH)

        @block.tensor
        def _(pe):
            pe.wait_ge(weights_in, 16 * 10)
            for i in range(3):
                last = nc.tensor.transpose(spare[:, E * i:E * i + E], wff[:, i, :], ident)
            last.then_inc(setup_pe, 1)
            pe.wait_ge(setup_act, 1)
            pe.wait_ge(setup_dve, 1)
            for i in range(3):
                last = nc.tensor.matmul(spare[:, i:i + 1], rowsp[:, i, :], ones[:, 0:1], start=True, stop=True)
            last.then_inc(setup_pe, 1)
            pe.wait_ge(setup_act, 2)
            nc.tensor.matmul(spare[:, E:2 * E], ones[:], rows[:, 3 * E:], start=True, stop=False)
            nc.tensor.matmul(spare[:, E:2 * E], vcol[:].to_broadcast([E, P]), wp[:], start=False, stop=True)\
                .then_inc(setup_pe, 1)
            pe.wait_ge(armed, 1)

            def rowmax_transpose(par, half):
                src = rowmax[:, par, QUARTET * half:QUARTET * half + QUARTET, :].rearrange("p a b -> p (a b)")
                return nc.tensor.transpose(spare[0:MAXIMA, 0:P], src, ident)

            def tokens_by_weights(tokensT, weights):
                for t in range(TT):
                    last = nc.tensor.matmul(spare[:, P * t:P * t + P], tokensT[:, P * t:P * t + P], weights,
                                            start=True, stop=True)
                return last

            def spare_use(b, par, g, place):
                stage, use = SPARE_USES.get((g, place), (None, None))
                if stage is None or not active(stage, b):
                    return
                wait(pe, spare_read, spare_before(b, use))
                if use == "xT":
                    wait(pe, xa_in, 16 * (before("X", b) + 1))
                    for t in range(TT):
                        last = nc.tensor.transpose(spare[:, P * t:P * t + P], xa[:, t, :], ident)
                elif use in ("q", "k"):
                    last = nc.tensor.matmul(spare[:], w1p[:, "qk".index(use), :], xT[:, par], start=True, stop=True)
                elif use == "v":
                    last = tokens_by_weights(xT[:, 1 - par], w1p[:, 2, :])
                elif use == "max0":
                    wait(pe, s_reduced, 4 * GROUPS * before("S", b) + 2 * GROUPS)
                    last = rowmax_transpose(1 - par, 0)
                elif use == "max1":
                    wait(pe, s_reduced, 4 * GROUPS * (before("T", b) + 1))
                    last = rowmax_transpose(par, 1)
                elif use in ("sums0", "sums1"):
                    half = int(use[-1])
                    wait(pe, o_copied, 2 * before(stage, b) + half + 1)
                    for t in range(TT):
                        last = nc.tensor.transpose(spare[:, P * t:P * t + P], osum[:, half, P * t:P * t + P], ident)
                elif use == "attnT":
                    for t in range(TT):
                        last = nc.tensor.transpose(spare[:, P * t:P * t + P],
                                                   attn[:, t].rearrange("q h d -> q (h d)"), ident)
                elif use == "project":
                    last = tokens_by_weights(attnT, wp[:])
                elif use == "hT":
                    wait(pe, h_done, before("D", b) + 1)
                    for t in range(TT):
                        last = nc.tensor.transpose(spare[:, P * t:P * t + P], h[:, 1 - par, t, :], ident)
                elif use == "key":
                    wait(pe, mixed_done, 2 * (before("E", b) + 1))
                    last = nc.tensor.matmul(spare[:], wffT[:, 1, :], mixed[:, 1, :], start=True, stop=True)
                elif use == "gate":
                    last = tokens_by_weights(mixed[:, 0], wffT[:, 0, :])
                elif use == "value":
                    wait(pe, ksq_done, before("E", b) + 1)
                    last = tokens_by_weights(ksq, wffT[:, 2, :])
                last.then_inc(spare_written, 1)

            def t_chunk(b, par, g, i):
                n = 4 * GROUPS * before("T", b) + 4 * g + i
                half, c = divmod(g, CHUNKS)
                if c == 0 and i == 0:
                    wait(pe, max_in[half], 32 * (before("T", b) + 1))
                wait(pe, exp_done, bank_free(n, QUARTET * g + i))
                for t, hh, a, off, w in exp_chunk(c, i):
                    pair = QUARTET * half + t
                    r = slice(HROWS * hh, HROWS * hh + TERMS + MROWS)
                    last = nc.tensor.matmul(tps[:, bank(QUARTET * g + i), off:off + w], kop[r, par, pair, BLK * a:BLK * a + BLK],
                                            qop[r, par, pair, BLK * a:SEQ], start=True, stop=True)
                last.then_inc(t_done, 1)

            def s_chunk(b, par, g, i):
                n = 4 * GROUPS * before("S", b) + 4 * g + i
                half, c = divmod(g, CHUNKS)
                if c == 0 and i == 0:
                    wait(pe, ops_in[half], LOADED * (before("S", b) + 1))
                wait(pe, s_reduced, bank_free(n, QUARTET * g + i))
                pair = QUARTET * half + i
                blocks = max_chunk(c)
                for j, (a, off, w) in enumerate(blocks):
                    for hh in range(2):
                        r = slice(HROWS * hh, HROWS * hh + TERMS)
                        nc.tensor.matmul(sps[HROWS * hh:HROWS * hh + QBLK, bank(QUARTET * g + i), off:off + w],
                                         qop[r, par, pair, QBLK * a:QBLK * a + QBLK],
                                         kop[r, par, pair, 0:w], start=j == 0, stop=False,
                                         skip_group_check=True)
                for j, (a, off, w) in enumerate(blocks):
                    last = nc.tensor.matmul(sps[:, bank(QUARTET * g + i), off + w - QBLK:off + w], dup[:], qmask[:],
                                            start=False, stop=j == len(blocks) - 1, skip_group_check=True)
                last.then_inc(s_done, 1)

            def pv(b, entries, par, g):
                half, c = divmod(g, CHUNKS)
                if c == 0:
                    wait(pe, o_copied, 2 * entries + half)
                    if half == 0:
                        wait(pe, spare_read, last_use(b, "v"))
                wait(pe, masked, GROUPS * entries + g + 1)
                by_pair = sorted((t, hh, j, i) for i in range(QUARTET)
                                 for j, (t, hh, _, _, _) in enumerate(exp_chunk(c, i)))
                per_pair = len(by_pair) // QUARTET
                for k in range(per_pair):
                    for t in range(QUARTET):
                        _, hh, j, i = by_pair[per_pair * t + k]
                        _, _, a, off, w = exp_chunk(c, i)[j]
                        last = nc.tensor.matmul(ops[32 * t:32 * t + 32, BLK * a:SEQ],
                                                vop[:, par, a, QUARTET * half + t, hh, :],
                                                probs[:, g % 2, i, off:off + w],
                                                start=c == 0, stop=c == CHUNKS - 1, skip_group_check=True)
                last.then_inc(pv_done, 1)

            def step(b, par):
                for g in range(GROUPS):
                    for i in range(QUARTET):
                        if active("T", b):
                            t_chunk(b, par, g, i)
                        if active("S", b):
                            s_chunk(b, 1 - par, g, i)
                        if i % 2 == 1:
                            spare_use(b, par, g, i // 2)
                    if g == 0 and active("D", b):
                        pv(b, before("D", b), 1 - par, GROUPS - 1)
                    elif g > 0 and active("T", b):
                        pv(b, before("T", b), par, g - 1)

            run_steps(pe, step)

        @block.scalar
        def _(act):
            act.wait_ge(setup_pe, 1)
            nc.scalar.copy(wffT[:, 0:2].rearrange("p a b -> p (a b)"), spare[:, 0:2 * E])
            nc.scalar.activation(wffT[:, 2, :], spare[:, 2 * E:3 * E], ACT.Copy, scale=0.5).then_inc(setup_act, 1)
            act.wait_ge(setup_pe, 2)
            nc.scalar.copy(bias[:, 0:2], spare[:, 0:2])
            nc.scalar.copy(vcol[:], spare[:, 2:3]).then_inc(setup_act, 1)
            act.wait_ge(setup_pe, 3)
            nc.scalar.copy(bias[:, E:2 * E], spare[:, E:2 * E]).then_inc(setup_act, 1)
            act.wait_ge(setup_act, 3)
            act.wait_ge(armed, 1)

            def spare_use(b, par, g, place):
                stage, use = SPARE_USES.get((g, place), (None, None))
                if stage is None or not active(stage, b) or use in ("sums0", "sums1", "project", "value"):
                    return
                n = before(stage, b)
                if use in ("max0", "max1"):
                    m = 2 * n + (0 if use == "max0" else 1)
                    wait(act, max_split, m)
                wait(act, spare_written, spare_before(b, use) + 1)
                if use == "xT":
                    ins = nc.scalar.copy(xT[:, 1 - par], spare[:])
                elif use == "v":
                    if is_static(b) and n == 0:
                        act.wait_ge(vop_cleared, 2)
                    wait(act, pv_done, GROUPS * before("T", b))
                    for hh in range(2):
                        ins = nc.scalar.copy(vop[:, 1 - par, :, :, hh, DH * hh:DH * hh + DH],
                                             spare[:].rearrange("k (t p h d) -> k h t p d", t=TT, p=PAIRS, h=2)[:, hh])
                elif use == "attnT":
                    ins = nc.scalar.copy(attnT[:], spare[:])
                elif use in ("q", "k"):
                    i = "qk".index(use)
                    wait(act, parts_out, 16 * n)
                    nc.scalar.activation(part(i, 0), spare[:], ACT.Identity, bias=bias[:, i:i + 1])\
                        .then_inc(qk_high, 1)
                    return
                elif use in ("max0", "max1"):
                    ins = nc.scalar.activation(negmax[:], spare[0:MAXIMA, 0:P], ACT.Copy, scale=-1.0)
                elif use == "hT":
                    wait(act, mixed_done, 2 * n)
                    ins = nc.scalar.copy(hT[:, 1:SEQ + 1], spare[:])
                elif use == "key":
                    wait(act, ksq_done, n)
                    ins = nc.scalar.activation(krelu[:], spare[:], ACT.Relu)
                elif use == "gate":
                    ins = nc.scalar.activation(gate[:], spare[:], ACT.Tanh, scale=0.5)
                ins.then_inc(spare_read, 1)

            def exp_chunk_of(b, g, i):
                n = before("T", b)
                half, c = divmod(g, CHUNKS)
                if i == 0:
                    wait(act, pv_done, GROUPS * n + g - 1)
                wait(act, t_done, 4 * GROUPS * n + 4 * g + i + 1)
                nc.scalar.activation(probs[:, g % 2, i, :], tps[:, bank(QUARTET * g + i), :], ACT.Exp, scale=SCALE)\
                    .then_inc(exp_done, 1)

            def copy_o(n, half, taken):
                wait(act, spare_written, taken)
                wait(act, pv_done, GROUPS * n + CHUNKS * (half + 1))
                nc.scalar.copy(osum[:, half, :], ops[:]).then_inc(o_copied, 1)

            def split_middle(b, i):
                n = 2 * before("A", b) + i
                wait(act, spare_read, spare_before(b, "qk"[i]) + 1)
                nc.scalar.copy(part(i, 1), qk_rest[:, i, :]).then_inc(qk_middle, 1)

            def scale_steps(n):
                wait(act, step_done, n + 1)
                wait(act, mixed_done, 2 * n)
                for i in range(2):
                    nc.scalar.activation(scaled[:, i, :], step_d[:], ACT.Copy, scale=mus[:, i:i + 1])\
                        .then_inc(scaled_done, 1)

            def step(b, par):
                for g in range(GROUPS):
                    if active("T", b):
                        exp_chunk_of(b, g, 0)
                        exp_chunk_of(b, g, 1)
                    spare_use(b, par, g, 0)
                    if g == 1 and active("D", b):
                        copy_o(before("D", b), 1, last_use(b, "sums1"))
                    if g == CHUNKS + 1 and active("T", b):
                        copy_o(before("T", b), 0, last_use(b, "sums0"))
                    if active("T", b):
                        exp_chunk_of(b, g, 2)
                        exp_chunk_of(b, g, 3)
                    spare_use(b, par, g, 1)
                    if g in (1, 2) and active("A", b):
                        split_middle(b, g - 1)
                    if g == 9 and active("D", b):
                        scale_steps(before("D", b))

            run_steps(act, step)

        @block.vector
        def _(dve):
            nc.vector.memset(ones[:], 1.0)
            nc.vector.memset(hT[:, 0:1], 0.0)
            dve.wait_ge(weights_in, 16 * 10)
            nc.vector.tensor_copy(dup[:], cst[0:QBLK, C_DUP:C_DUP + P])
            nc.vector.tensor_copy(qmask[:], cst[0:QBLK, C_MASK:C_MASK + QBLK])
            for i in range(3):
                order = "c (h p d) -> c h p d" if i < 2 else "c (p h d) -> c h p d"
                nc.vector.tensor_copy(
                    w1p[:, i, :].rearrange(order, h=2, d=DH),
                    w1[:].rearrange("c (p h i d) -> c i h p d", h=2, i=3, d=DH)[:, i])
                last = nc.vector.tensor_copy(
                    rowsp[:, i, :].rearrange(order, h=2, d=DH),
                    rows[:, 0:3 * E].rearrange("c (p h i d) -> c i h p d", h=2, i=3, d=DH)[:, i])
            last.then_inc(setup_dve, 1)
            dve.wait_ge(setup_dve, 1)
            dve.wait_ge(setup_act, 3)
            nc.vector.memset(half_power[:], -0.5).then_inc(armed, 1)

            def reduce_chunk(b, par, g, i):
                n = 4 * GROUPS * before("S", b) + 4 * g + i
                half, c = divmod(g, CHUNKS)
                wait(dve, s_done, n + 1, alone=False)
                for a, off, w in max_chunk(c):
                    last = nc.vector.reduce_max(rowmax[:, par, QUARTET * half + i, a:a + 1],
                                                sps[:, bank(QUARTET * g + i), off:off + w], axis=AX_X)
                last.then_inc(s_reduced, 1)

            def layer_norm_moments(src, i, n, ready, value, done_stats, done_moments):
                wait(dve, ready, value)
                for t in range(TT):
                    last = nc.vector.bn_stats(out=stats[:, i, t, :], in_=src[:, t, :])
                last.then_inc(done_stats, 1)
                wait(dve, done_stats, n + 1)
                for t in range(TT):
                    last = nc.vector.bn_aggr(out=moments[:, i, t, :], in_=stats[:, i, t, :])
                last.then_inc(done_moments, 1)

            def spare_use(b, par, g, place):
                stage, use = SPARE_USES.get((g, place), (None, None))
                if stage is None or not active(stage, b):
                    return
                n = before(stage, b)
                written = spare_before(b, use) + 1
                if use in ("q", "k"):
                    i = "qk".index(use)
                    wait(dve, qk_high, 2 * n + i + 1)
                    wait(dve, qk_split, 2 * (n - 1) + i + 1)
                    nc.vector.scalar_tensor_tensor(qk_rest[:, i, :], spare[:], bias[:, i:i + 1], part(i, 0),
                                                   ALU.add, ALU.subtract).then_inc(spare_read, 1)
                elif use in ("sums0", "sums1"):
                    half = int(use[-1])
                    wait(dve, spare_written, written)
                    tiles = spare[:].rearrange("q (t r s h d) -> q s t r h d", t=TT, r=QUARTET, s=2, h=2)
                    nc.vector.reciprocal(inv[:, half], tiles[:, 1, :, :, :, 0]).then_inc(inv_done, 1)
                    wait(dve, inv_done, 2 * n + half + 1)
                    for t in range(TT):
                        last = nc.vector.tensor_tensor(
                            attn[:, t, DH * half:DH * half + DH].rearrange("q (r h) d -> q r h d", h=2),
                            tiles[:, 0, t], inv[:, half, t].unsqueeze(3).to_broadcast([P, QUARTET, 2, DH]), ALU.mult)
                    last.then_inc(spare_read, 1)
                elif use == "project":
                    wait(dve, xbias_done, n + 1)
                    wait(dve, h_done, n)
                    wait(dve, spare_written, written)
                    nc.vector.tensor_tensor(y[:].rearrange("p t e -> p (t e)"), spare[:],
                                            xbias[:].rearrange("p t e -> p (t e)"), ALU.add).then_inc(spare_read, 1)
                elif use == "value":
                    wait(dve, z_done, n)
                    wait(dve, spare_written, written)
                    nc.vector.scalar_tensor_tensor(gated[:], gate[:], 1.0, spare[:], ALU.add, ALU.mult)\
                        .then_inc(spare_read, 1)

            def normalise(i, n, src, dst, done_rstd, done):
                wait(dve, done_rstd, n + 1)
                for t in range(TT):
                    last = nc.vector.tensor_scalar(dst[:, t, :], src[:, t, :], moments[:, i, t, 0:1],
                                                   rstd[:, i, t:t + 1], ALU.subtract, ALU.mult)
                last.then_inc(done, 1)

            def step(b, par):
                for g in range(GROUPS):
                    if active("S", b):
                        reduce_chunk(b, 1 - par, g, 0)
                        reduce_chunk(b, 1 - par, g, 1)
                    spare_use(b, par, g, 0)
                    if g == 7 and active("D", b):
                        wait(dve, z_done, before("E", b))
                        normalise(0, before("D", b), y, h[:, 1 - par], rstd_done, h_done)
                    if g == 9 and active("E", b):
                        n = before("E", b)
                        wait(dve, stored, 16 * n)
                        normalise(1, n, z, result, rstd2_done, result_done)
                    if g == 5 and active("D", b):
                        layer_norm_moments(y, 0, before("D", b), spare_read, spare_before(b, "project") + 1,
                                           stats_done, moments_done)
                    if g == 6 and active("E", b):
                        layer_norm_moments(z, 1, before("E", b), z_done, before("E", b) + 1, stats2_done, moments2_done)
                    if active("S", b):
                        reduce_chunk(b, 1 - par, g, 2)
                        reduce_chunk(b, 1 - par, g, 3)
                    spare_use(b, par, g, 1)

            run_steps(dve, step)

        @block.gpsimd
        def _(pool):
            nc.gpsimd.memset(vop[:], 0.0).then_inc(vop_cleared, 1)
            nc.gpsimd.memset(kop[:], 1.0).then_inc(kop_cleared, 1)
            pool.wait_ge(vop_cleared, 1)
            for hh in range(2):
                last = nc.gpsimd.memset(vop[:].rearrange("k b t p h c -> k (b t p) h c")[
                    :, :, hh, (2 + hh) * DH:(3 + hh) * DH], 1.0)
            last.then_inc(vop_cleared, 1)
            pool.wait_ge(armed, 1)

            def mask_group(b, g):
                n = before("T", b)
                wait(pool, exp_done, 4 * GROUPS * n + 4 * g + 4)
                for _, _, _, off, _ in exp_chunk(g % CHUNKS, 0):
                    v = probs[:, g % 2, :, off:off + BLK]
                    last = nc.gpsimd.affine_select(out=v, in_=v, compare_op=ALU.is_ge, fill=0.0, base=0,
                                                   pattern=[[0, QUARTET], [1, BLK]], channel_multiplier=-1)
                last.then_inc(masked, 1)

            def split_low(b, i):
                wait(pool, qk_middle, 2 * before("A", b) + i + 1)
                nc.gpsimd.tensor_tensor(part(i, 2), qk_rest[:, i, :], part(i, 1), ALU.subtract).then_inc(qk_split, 1)

            def split_max(n, b, use):
                wait(pool, spare_read, spare_before(b, use) + 1)
                wait(pool, max_out, 16 * n)
                nc.gpsimd.tensor_scalar(negmax_parts[:, 0, :], negmax[:], 1.0, 0.0, ALU.mult, ALU.add).then_inc(max_high, 1)
                wait(pool, max_high, n + 1)
                nc.gpsimd.tensor_tensor(negmax_parts[:, 1, :], negmax[:], negmax_parts[:, 0, :], ALU.subtract)\
                    .then_inc(max_split, 1)

            def inverse_deviation(i, n, done_moments, done_eps, done_rstd):
                wait(pool, done_moments, n + 1)
                nc.gpsimd.tensor_scalar(vareps[:, i, :], moments[:, i, :, 1], EPS, None, ALU.add).then_inc(done_eps, 1)
                wait(pool, done_eps, n + 1)
                nc.gpsimd.tensor_tensor(rstd[:, i, :], vareps[:, i, :], half_power[:], ALU.pow).then_inc(done_rstd, 1)

            def mix_step(n, b):
                wait(pool, spare_read, spare_before(b, "hT") + 1)
                nc.gpsimd.tensor_tensor(step_d[:], hT[:, 1:SEQ + 1], hT[:, 0:SEQ], ALU.subtract)\
                    .then_inc(step_done, 1)

            def mix_sum(n):
                for i in range(2):
                    wait(pool, scaled_done, 2 * n + i + 1)
                    nc.gpsimd.tensor_tensor(mixed[:, i, :], scaled[:, i, :], hT[:, 0:SEQ], ALU.add)\
                        .then_inc(mixed_done, 1)

            def step(b, par):
                for g in range(GROUPS):
                    if g == 0 and active("E", b):
                        mix_sum(before("E", b))
                    if g == 3 and active("E", b):
                        wait(pool, spare_read, spare_before(b, "key") + 1)
                        nc.gpsimd.tensor_tensor(ksq[:], krelu[:], krelu[:], ALU.mult).then_inc(ksq_done, 1)
                    if g == 2 and active("T", b):
                        split_max(2 * before("T", b) + 1, b, "max1")
                    if g in (2, 3) and active("A", b):
                        split_low(b, g - 2)
                    if g == 3 and active("D", b):
                        n = before("D", b)
                        wait(pool, xres_in, 16 * (n + 1))
                        wait(pool, h_done, n)
                        nc.gpsimd.tensor_tensor(xbias[:], xres[:],
                                                bias[:, E:2 * E].unsqueeze(1).to_broadcast([P, TT, E]),
                                                ALU.add).then_inc(xbias_done, 1)
                    if g == 5 and active("E", b):
                        n = before("E", b)
                        wait(pool, spare_read, spare_before(b, "value") + 1)
                        wait(pool, result_done, n)
                        nc.gpsimd.tensor_tensor(z[:].rearrange("p t e -> p (t e)"), gated[:],
                                                h[:, par].rearrange("p t e -> p (t e)"), ALU.add).then_inc(z_done, 1)
                    if g == 6 and active("D", b):
                        inverse_deviation(0, before("D", b), moments_done, vareps_done, rstd_done)
                    if g == 7 and active("E", b):
                        inverse_deviation(1, before("E", b), moments2_done, vareps2_done, rstd2_done)
                    if g == 7 and active("S", b):
                        split_max(2 * before("S", b), b, "max0")
                    if g == 9 and active("D", b):
                        mix_step(before("D", b), b)
                    if active("T", b):
                        mask_group(b, g)

            run_steps(pool, step)


def shape_constants(np):
    c = np.zeros((P, C_END), np.float32)
    c[:, C_IDENT:C_IDENT + P] = np.eye(P)
    c[0:QBLK, C_DUP:C_DUP + P] = np.tile(np.eye(QBLK), (1, 2))
    c[0:QBLK, C_MASK:C_MASK + QBLK] = np.triu(np.full((QBLK, QBLK), MASKED), 1)
    return c


INPUTS = ["L0_attn_x", "L0_attn_W1", "L0_attn_b1", "L0_attn_Wp", "L0_attn_bp",
          "L0_ffn_W_r", "L0_ffn_W_k", "L0_ffn_W_v", "L0_ffn_mu_r", "L0_ffn_mu_k"]


def kernel(**inputs):
    import numpy as np
    import concourse.bacc as bacc
    from concourse.bass_utils import run_bass_kernel_spmd

    nc = bacc.Bacc("TRN2", target_bir_lowering=False, num_devices=1)
    arrays = {name: np.ascontiguousarray(inputs[name]) for name in INPUTS}
    arrays["shape_constants"] = shape_constants(np)
    args = [nc.dram_tensor(name, a.shape, mybir.dt.from_np(a.dtype), kind="ExternalInput").ap()
            for name, a in arrays.items()]
    args.append(nc.dram_tensor("out", (BATCH, SEQ, E), F32, kind="ExternalOutput").ap())
    block_program(nc, *args)
    return run_bass_kernel_spmd(nc, [arrays], core_ids=[0]).results[0]["out"]
```
